# Optimizing a Trainium2 kernel written in Bass

```python
import numpy as np
import jax
import jax.numpy as jnp

def _softmax(x, axis=-1):
    return jax.nn.softmax(x, axis=axis)

def _gelu(x):
    return jax.nn.gelu(x, approximate=True)

def _silu(x):
    return jax.nn.silu(x)

def _sigmoid(x):
    return jax.nn.sigmoid(x)

def _layernorm(x, axis=-1, eps=1e-05):
    m = jnp.mean(x, axis=axis, keepdims=True)
    v = jnp.var(x, axis=axis, keepdims=True)
    return (x - m) / jnp.sqrt(v + eps)

def _scatter_add(tgt, idx, src, axis=0):
    return tgt.at[idx].add(src)

def _segment_sum(src, seg, n):
    return jax.ops.segment_sum(src, seg, n)
kernel_name = 'mk_adj_preln_d1_adj_r2_a96294'

def setup_inputs(seed: int=0):
    np.random.seed(seed)
    _w = jnp.asarray

    def _rec_inputs():
        import jax
        import jax.numpy as jnp
        _gk = jax.random.key(seed)
        x = -0.0005207 + 1.001 * jax.random.normal(jax.random.fold_in(_gk, 1), (4096, 128), jnp.float32)
        _a = jax.random.bernoulli(jax.random.fold_in(_gk, 2), 0.00195312, (4096, 4096))
        adj = _a.astype(jnp.int32)
        return (x, adj)
    x, adj = _rec_inputs()

    def _L0_gnn_setup():
        import jax, jax.numpy as jnp
        import numpy as np
        MIN_NORM = 1e-15
        EPS = 1e-07
        MASK_FILL = -9000000000000000.0

        def logmap0(x, c):
            K = 1.0 / c
            sqrtK = K ** 0.5
            y = x[:, 1:]
            y_norm = jnp.clip(jnp.linalg.norm(y, axis=-1, keepdims=True), MIN_NORM)
            theta = jnp.clip(x[:, :1] / sqrtK, 1.0 + EPS)
            res = sqrtK * jnp.arccosh(theta) * y / y_norm
            return jnp.concatenate([jnp.zeros_like(x[:, :1]), res], axis=1)

        def proj(x, c):
            K = 1.0 / c
            y = x[:, 1:]
            x0 = jnp.sqrt(K + jnp.sum(y * y, axis=-1, keepdims=True))
            return jnp.concatenate([x0, y], axis=1)

        def expmap0(u, c):
            K = 1.0 / c
            sqrtK = K ** 0.5
            x = u[:, 1:]
            x_norm = jnp.clip(jnp.linalg.norm(x, axis=-1, keepdims=True), MIN_NORM)
            theta = x_norm / sqrtK
            res = jnp.concatenate([sqrtK * jnp.cosh(theta), sqrtK * jnp.sinh(theta) * x / x_norm], axis=1)
            return proj(res, c)
        key = jax.random.key(seed)
        k1, k2, k3, k4, k5 = jax.random.split(key, 5)
        N, D_in, D_out = (4096, 128, 128)
        x = jax.random.normal(k1, (N, D_in), dtype=jnp.float32)
        adj = jax.random.randint(k2, (N, N), 0, 2, dtype=jnp.int32)
        W_gcn = jax.random.normal(k3, (D_in - 1, D_out - 1), dtype=jnp.float32)
        std_w = 1.414 * (2.0 / (D_out + D_out)) ** 0.5
        W_att = jax.random.normal(k4, (D_out, D_out), dtype=jnp.float32) * std_w
        std_a = 1.414 * (2.0 / (2 * D_out + 1)) ** 0.5
        a_att = jax.random.normal(k5, (2 * D_out, 1), dtype=jnp.float32) * std_a
        return {'x': x, 'adj': adj, 'k': 1, 'W_gcn': W_gcn, 'W_att': W_att, 'a_att': a_att}
    _L0_gnn_all = _L0_gnn_setup()
    _L0_gnn_in = {k: v for k, v in _L0_gnn_all.items() if k in ('W_gcn', 'W_att', 'a_att')}
    del _L0_gnn_all
    return {'x': x, 'adj': adj, 'L0_gnn_W_gcn': _L0_gnn_in['W_gcn'], 'L0_gnn_W_att': _L0_gnn_in['W_att'], 'L0_gnn_a_att': _L0_gnn_in['a_att']}

def reference(x, adj, L0_gnn_W_gcn, L0_gnn_W_att, L0_gnn_a_att):
    import jax
    import jax.numpy as jnp

    def _L0_gnn_ref(x, adj, k, W_gcn, W_att, a_att):
        import jax, jax.numpy as jnp
        import numpy as np
        MIN_NORM = 1e-15
        EPS = 1e-07
        MASK_FILL = -9000000000000000.0

        def logmap0(x, c):
            K = 1.0 / c
            sqrtK = K ** 0.5
            y = x[:, 1:]
            y_norm = jnp.clip(jnp.linalg.norm(y, axis=-1, keepdims=True), MIN_NORM)
            theta = jnp.clip(x[:, :1] / sqrtK, 1.0 + EPS)
            res = sqrtK * jnp.arccosh(theta) * y / y_norm
            return jnp.concatenate([jnp.zeros_like(x[:, :1]), res], axis=1)

        def proj(x, c):
            K = 1.0 / c
            y = x[:, 1:]
            x0 = jnp.sqrt(K + jnp.sum(y * y, axis=-1, keepdims=True))
            return jnp.concatenate([x0, y], axis=1)

        def expmap0(u, c):
            K = 1.0 / c
            sqrtK = K ** 0.5
            x = u[:, 1:]
            x_norm = jnp.clip(jnp.linalg.norm(x, axis=-1, keepdims=True), MIN_NORM)
            theta = x_norm / sqrtK
            res = jnp.concatenate([sqrtK * jnp.cosh(theta), sqrtK * jnp.sinh(theta) * x / x_norm], axis=1)
            return proj(res, c)
        c = float(k)
        N = x.shape[0]
        logx = logmap0(x, c)
        Wx = logx[:, 1:] @ W_gcn
        tmp = jnp.concatenate([jnp.zeros((N, 1), x.dtype), Wx], axis=1)
        fun7 = proj(expmap0(tmp, c), c)
        h_in = logmap0(fun7, c)
        h = h_in @ W_att
        F_ = h.shape[1]
        e = h @ a_att[:F_] + (h @ a_att[F_:]).T
        att = jnp.where(adj > 0, e, MASK_FILL)
        att = jax.nn.softmax(att, axis=1)
        h_prime = att @ h
        emb = jax.nn.elu(h_prime)
        emb = proj(emb, c)
        out = expmap0(jax.nn.sigmoid(logmap0(emb, c)), c)
        return out
    h = jnp.maximum(_layernorm(x, axis=-1), 0.0)
    x = x + _L0_gnn_ref(h, adj, 1, L0_gnn_W_gcn, L0_gnn_W_att, L0_gnn_a_att)
    return x

_drawn_inputs = setup_inputs


def setup_inputs(seed=0):
    import zlib

    import numpy as np

    out = dict(_drawn_inputs(seed))
    spreads = {}
    factors = {}
    for name, (base, spread) in spreads.items():
        noise = np.random.default_rng([zlib.crc32(name.encode()), seed]).standard_normal(out[name].shape)
        drawn = base * np.exp(spread * noise) if base else spread * noise
        out[name] = jnp.asarray(drawn.astype(out[name].dtype))
    for name, factor in factors.items():
        out[name] = (out[name] * factor).astype(out[name].dtype)
    return out
```

```python
import math
from contextlib import ExitStack

import concourse.bass as bass
from concourse import mybir

N, D = 4096, 128
P = 128
NB = N // P
CW = 512
CB = CW // P
NC = N // CW
TJ = 4
NT = NB // TJ
SLOTS = 2 * NT
MASKS = 4
XG = 4
GB = NB // XG
LN_EPS = 1e-5
EPS = 2.0 ** -23
S_EPS = math.sqrt(EPS * (EPS + 2.0))
NORM2_MIN = 1e-30
ROOT_SCALE = 2.0 ** 40
HALF_ROOT = 2.0 ** -21
MASK_FILL = -9000000000000000.0
SHIFT = 60.0
RANGE_LIMIT = 125.0
SPLIT_SCALE = 512.0

DVE_STEPS = ["flag", "rden", "em", "y0", "y1", "y2", "y3",
             "q", "lift", "one_q", "re", "quot", "root", "xp", "rxp", "u", "m", "w", "ryn",
             "f", "ssq", "ns", "re2", "quot2", "root2", "rn", "ren", "diff", "F", "hsum",
             "o0", "o1", "o2", "o3", "col0"]
ACT_STEPS = ["acc", "e0", "e1", "e2", "e3", "sq_y", "ln1", "exp1", "ln_w",
             "s0", "s1", "s2", "s3", "sq_s", "ln2", "exp2", "exp_n"]
V = {n: i + 1 for i, n in enumerate(DVE_STEPS)}
A = {n: i + 1 for i, n in enumerate(ACT_STEPS)}
NV, NA = len(DVE_STEPS), len(ACT_STEPS)


def build(nc, x, adj_t, w_gcn, w_gcn_t, w_att, w_att_t, a2, out):
    f32, bf16, f16, i32 = mybir.dt.float32, mybir.dt.bfloat16, mybir.dt.float16, mybir.dt.int32
    ALU, ACT, AX = mybir.AluOpType, mybir.ActivationFunctionType, mybir.AxisListType

    x_src = x.rearrange("(p b) d -> p b d", b=NB)
    x_rows = x.rearrange("(c p b) d -> c p b d", p=P, b=CB)
    out_rows = out.rearrange("(c p b) d -> c p b d", p=P, b=CB)

    with ExitStack() as ctx:
        def sb(name, shape, dt):
            return ctx.enter_context(nc.sbuf_tensor(name, shape, dt))

        def sem(name):
            return ctx.enter_context(nc.semaphore(name))

        raw = sb("raw", [P, SLOTS, TJ * CW], i32)
        stage = sb("stage", [P, NB * D], f32)
        z = stage[:, :].rearrange("p (b d) -> p b d", d=D)
        mask = stage[:, :].bitcast(bf16).rearrange("p (s j i) -> p s j i", s=MASKS, j=TJ)
        H = sb("H", [P, NB, D], f32)
        hi = sb("hi", [P, NB, D], f16)
        lo = sb("lo", [P, NB, D], f16)

        def raw_f32(first, slots):
            return raw[:, first:first + slots, :].rearrange("p s n -> p (s n)").bitcast(f32)

        zT = raw_f32(SLOTS - 6, 2).rearrange("p (b d) -> p b d", d=D)
        sqH = raw_f32(SLOTS - 4, 2).rearrange("p (b d) -> p b d", d=D)
        sqz = raw_f32(SLOTS - 2, 2).rearrange("p (b d) -> p b d", d=D)

        accS = sb("accS", [P, CW], f32)
        E = sb("E", [P, CB, D], f32)
        y = sb("y", [P, CB, D], f32)
        sq = sb("sq", [P, CB, D], f32)
        sig = sb("sig", [P, CB, D], f32)
        x_res = [sb(f"x_res{i}", [P, CB, D], f32) for i in range(2)]
        o = [sb(f"o{i}", [P, CB, D], f32) for i in range(2)]

        ident = sb("ident", [P, P], f32)
        wg = sb("wg", [P, P], f32)
        wgT = sb("wgT", [P, P], f32)
        wa = sb("wa", [P, P], f32)
        waT = sb("waT", [P, P], f32)
        a2s = sb("a2s", [P, 1], f32)
        v_sb = sb("v_sb", [P, 1], f32)
        ones_row = sb("ones_row", [1, P], f32)
        inv_n = sb("inv_n", [P, 1], f32)
        hmean = sb("hmean", [P, 1], f32)
        mean_row = sb("mean_row", [1, P], f32)
        empty = sb("empty", [1, CW], f32)
        stats = sb("stats", [P, NB, 6], f32)
        col = {n: sb("c_" + n, [P, NB], f32) for n in
               ["msum", "mean", "d", "m2", "ve", "lv", "r0", "rstd", "u1", "zq", "acosh1", "r",
                "wq", "n2", "ln_n", "e_n", "re_n", "root_n", "en", "ren", "sh2", "ch", "rch",
                "u", "w", "acosh2", "rn", "gr", "t", "p", "rw", "f"]}
        pair = sb("pair", [P, 2, NB], f32)
        pair_e = sb("pair_e", [P, 2, NB], f32)
        pair_r = sb("pair_r", [P, 2, NB], f32)
        w_bf = sb("w_bf", [P, NB], bf16)
        tmm = sb("tmm", [P, 2], f32)
        gmm = sb("gmm", [1, 2], f32)
        shift = sb("shift", [P, 1], f32)
        spread = sb("spread", [P, 1], f32)
        wide = sb("wide", [P, 1], i32)
        small = {n: sb("s_" + n, [P, CB], f32) for n in
                 ["rden", "q", "xp", "rxp", "u", "m", "w", "acosh", "ryn", "f", "ssq", "ns",
                  "ln2", "e2", "re2", "quot2", "root2", "rn", "en", "ren", "diff", "F", "hsum"]}
        sp = sb("sp", [P, 2, CB], f32)
        sp_e = sb("sp_e", [P, 2, CB], f32)
        sp_r = sb("sp_r", [P, 2, CB], f32)
        sp_s = sb("sp_s", [P, 2, CB], f32)
        rawG = raw[:, 0, :].rearrange("p (j i) -> p j i", j=TJ)
        eG = raw_f32(1, 1).rearrange("p (j i) -> p j i", j=TJ)
        fillG = raw_f32(2, 1).rearrange("p (j i) -> p j i", j=TJ)
        mixG = raw_f32(3, 1)
        pG = mixG[:, 0:CW].rearrange("p (b j) -> p b j", b=CB)
        pTG = mixG[:, CW:2 * CW]
        accG = mixG[:, 2 * CW:3 * CW]
        hG = mixG[:, 3 * CW:3 * CW + D]
        sG = raw_f32(NT, NT).rearrange("p (b j) -> p b j", b=CB)
        tG = sb("tG", [P, TJ], f32)
        nmG = sb("nmG", [P, CB], f32)

        bank = [ctx.enter_context(nc.psum_tensor(f"bank{i}", [P, CW], f32)) for i in range(8)]
        acc = [bank[0], bank[1]]
        Z = bank[2][:, :].rearrange("p (b d) -> p b d", d=D)
        misc = bank[7]
        tp_ring = bank[0:4]
        zw_ring = bank[4:7]

        x_in = [sem(f"x_in{g}") for g in range(XG)]
        raw_in = [sem(f"raw_in{s}") for s in range(SLOTS)]
        row_io = [sem(f"row_io{i}") for i in range(2)]
        const_in = sem("const_in")
        att_in = sem("att_in")
        const_done = sem("const_done")
        zero_done = sem("zero_done")
        ident_done = sem("ident_done")
        prep_dve = sem("prep_dve")
        prep_act = sem("prep_act")
        v_mm = sem("v_mm")
        v_copied = sem("v_copied")
        tp_done = sem("tp_done")
        zT_done = sem("zT_done")
        zw_done = sem("zw_done")
        H_done = sem("H_done")
        sqz_done = sem("sqz_done")
        sqH_done = sem("sqH_done")
        z_done = sem("z_done")
        H_scaled = sem("H_scaled")
        tmm_done = sem("tmm_done")
        tmmT_done = sem("tmmT_done")
        gmm_done = sem("gmm_done")
        gmm_all = sem("gmm_all")
        split_done = sem("split_done")
        wide_done = sem("wide_done")
        masked = sem("masked")
        mm_done = sem("mm_done")
        hsum_done = sem("hsum_done")
        hmean_done = sem("hmean_done")
        mrow_mm = sem("mrow_mm")
        mrow_done = sem("mrow_done")
        tail_dve = sem("tail_dve")
        tail_act = sem("tail_act")
        tail_mm = sem("tail_mm")
        g_raw = sem("g_raw")
        g_free = sem("g_free")
        g_step = sem("g_step")
        g_e = sem("g_e")
        g_tp = sem("g_tp")
        g_max = sem("g_max")
        g_exp = sem("g_exp")
        g_col = sem("g_col")
        g_colT = sem("g_colT")
        g_pT = sem("g_pT")
        g_mm = sem("g_mm")
        g_acc = sem("g_acc")

        block = ctx.enter_context(nc.Block())

        @block.sync
        def _(eng):
            for g in range(XG):
                eng.dma_start(z[:, g * GB:(g + 1) * GB, :],
                              x_src[:, g * GB:(g + 1) * GB, :]).then_inc(x_in[g], 16)

            def load_tile(c, s):
                eng.dma_start(raw[:, s, :], adj_t[c, s % NT]).then_inc(raw_in[s], 16)

            def load_rows(c, i):
                eng.dma_start(x_res[i][:, :, :], x_rows[c]).then_inc(row_io[i], 16)

            def store_rows(c, i):
                eng.wait_ge(tail_dve, NV * (c + 1))
                eng.dma_start(out_rows[c], o[i][:, :, :]).then_inc(row_io[i], 16)

            for s in range(NT):
                load_tile(0, s)
            load_rows(0, 0)
            load_rows(1, 1)
            for s in range(NT, SLOTS - 6):
                load_tile(1, s)
            eng.wait_ge(sqH_done, 2 * XG + 1)
            for s in range(SLOTS - 6, SLOTS):
                load_tile(1, s)

            def pair_of_chunks(m, first):
                for i in range(2):
                    c = m * 2 + i
                    for k in range(NT):
                        eng.wait_ge(masked, c * NT - 2 * NT + k + 1)
                        load_tile(c, i * NT + k)
                    if not (first and i == 0):
                        store_rows(c - 3, 1 - i)
                        load_rows(c - 1, 1 - i)

            pair_of_chunks(1, True)
            with eng.Fori(2, NC // 2) as m:
                pair_of_chunks(m, False)
            store_rows(NC - 3, (NC - 3) % 2)
            load_rows(NC - 1, (NC - 1) % 2)
            store_rows(NC - 2, 0)
            store_rows(NC - 1, 1)
            for i in range(2):
                eng.wait_ge(row_io[i], 16 * NC)

            eng.wait_ge(wide_done, 1)
            go = eng.value_load(wide[0:1, 0:1], min_val=0, max_val=1)
            with eng.If(go == 1):
                with eng.Fori(0, NC) as c:
                    eng.wait_ge(row_io[0], c * 32 + 16 * NC)
                    eng.dma_start(x_res[0][:, :, :], x_rows[c]).then_inc(row_io[0], 16)
                    with eng.Fori(0, NT) as k:
                        eng.wait_ge(g_free, c * NT + k + 1)
                        eng.dma_start(raw[:, 0, :], adj_t[c, k]).then_inc(g_raw, 16)
                    eng.wait_ge(tail_dve, c * NV + NV * (NC + 1))
                    eng.dma_start(out_rows[c], o[0][:, :, :]).then_inc(row_io[0], 16)
                eng.wait_ge(row_io[0], 16 * NC + 32 * NC)

        @block.gpsimd
        def _(eng):
            eng.memset(ident[:, :], 0.0).then_inc(ident_done, 1)
            eng.memset(wg[:, :], 0.0).then_inc(zero_done, 1)
            eng.memset(wgT[:, :], 0.0).then_inc(zero_done, 1)
            eng.memset(wa[:, :], 0.0).then_inc(zero_done, 1)
            eng.wait_ge(ident_done, 1)
            eng.affine_select(out=ident[:, :], in_=ident[:, :], compare_op=ALU.not_equal, fill=1.0,
                              base=0, pattern=[[-1, P]], channel_multiplier=1).then_inc(ident_done, 1)
            eng.memset(ones_row[:, :], 1.0).then_inc(const_done, 1)
            eng.memset(inv_n[:, :], 1.0 / N).then_inc(const_done, 1)
            eng.wait_ge(zero_done, 3)
            eng.memset(wa[0:1, 0:1], 1.0).then_inc(const_done, 1)

        def tail_vector(eng, stage_no, i, vb, ab, tb, io_val):
            s = small

            def own(name):
                eng.wait_ge(tail_dve, vb + V[name])

            if stage_no == 0:
                eng.wait_ge(tail_act, ab + A["acc"])
                eng.tensor_scalar(out=empty[:, :], in0=accS[0:1, :], scalar1=0.0, scalar2=None,
                                  op0=ALU.is_equal).then_inc(tail_dve, 1)
            if stage_no == 1:
                eng.wait_ge(tail_mm, tb + 1)
                eng.reciprocal(s["rden"][:, :], Z[:, :, 0]).then_inc(tail_dve, 1)
            if stage_no == 2:
                eng.wait_ge(tail_act, ab + A["e3"])
                eng.tensor_scalar(out=E[:, :, :], in0=E[:, :, :], scalar1=1.0, scalar2=-1.0,
                                  op0=ALU.min, op1=ALU.add).then_inc(tail_dve, 1)
                own("em")
                for b in range(CB):
                    eng.scalar_tensor_tensor(out=y[:, b, :], in0=Z[:, b, :], scalar=s["rden"][:, b:b + 1],
                                             in1=E[:, b, :], op0=ALU.mult, op1=ALU.max).then_inc(tail_dve, 1)
            if stage_no == 3:
                eng.wait_ge(tail_act, ab + A["sq_y"])
                eng.tensor_reduce(out=s["q"][:, :], in_=sq[:, :, 1:D], axis=AX.X, op=ALU.add).then_inc(tail_dve, 1)
                own("q")
                eng.tensor_scalar(out=sp[:, 0, :], in0=s["q"][:, :], scalar1=NORM2_MIN, scalar2=ROOT_SCALE,
                                  op0=ALU.max, op1=ALU.mult).then_inc(tail_dve, 1)
                eng.tensor_scalar(out=sp[:, 1, :], in0=s["q"][:, :], scalar1=1.0, scalar2=None,
                                  op0=ALU.add).then_inc(tail_dve, 1)
            if stage_no == 4:
                eng.wait_ge(tail_act, ab + A["exp1"])
                eng.reciprocal(sp_r[:, :, :], sp_e[:, :, :]).then_inc(tail_dve, 1)
                own("re")
                eng.tensor_tensor(sp_r[:, :, :], sp[:, :, :], sp_r[:, :, :], op=ALU.mult).then_inc(tail_dve, 1)
                own("quot")
                eng.tensor_tensor(sp_s[:, :, :], sp_e[:, :, :], sp_r[:, :, :], op=ALU.add).then_inc(tail_dve, 1)
                own("root")
                eng.tensor_scalar(out=s["xp"][:, :], in0=sp_s[:, 1, :], scalar1=0.5, scalar2=1.0,
                                  op0=ALU.mult, op1=ALU.add).then_inc(tail_dve, 1)
                own("xp")
                eng.reciprocal(s["rxp"][:, :], s["xp"][:, :]).then_inc(tail_dve, 1)
                own("rxp")
                eng.tensor_tensor(s["u"][:, :], s["q"][:, :], s["rxp"][:, :], op=ALU.mult).then_inc(tail_dve, 1)
                eng.tensor_scalar(out=s["m"][:, :], in0=sp_s[:, 0, :], scalar1=HALF_ROOT, scalar2=S_EPS,
                                  op0=ALU.mult, op1=ALU.max).then_inc(tail_dve, 1)
                own("m")
                eng.scalar_tensor_tensor(out=s["w"][:, :], in0=s["u"][:, :], scalar=EPS, in1=s["m"][:, :],
                                         op0=ALU.max, op1=ALU.add).then_inc(tail_dve, 1)
                eng.reciprocal(s["ryn"][:, :], sp_s[:, 0, :]).then_inc(tail_dve, 1)
            if stage_no == 5:
                eng.wait_ge(tail_act, ab + A["ln_w"])
                own("ryn")
                eng.scalar_tensor_tensor(out=s["f"][:, :], in0=s["acosh"][:, :], scalar=1.0 / HALF_ROOT,
                                         in1=s["ryn"][:, :], op0=ALU.mult, op1=ALU.mult).then_inc(tail_dve, 1)
            if stage_no == 6:
                eng.wait_ge(tail_act, ab + A["sq_s"])
                eng.tensor_reduce(out=s["ssq"][:, :], in_=sq[:, :, 1:D], axis=AX.X, op=ALU.add).then_inc(tail_dve, 1)
                own("ssq")
                eng.tensor_scalar(out=s["ns"][:, :], in0=s["ssq"][:, :], scalar1=NORM2_MIN, scalar2=ROOT_SCALE,
                                  op0=ALU.max, op1=ALU.mult).then_inc(tail_dve, 1)
            if stage_no == 7:
                eng.wait_ge(tail_act, ab + A["exp2"])
                eng.reciprocal(s["re2"][:, :], s["e2"][:, :]).then_inc(tail_dve, 1)
                own("re2")
                eng.tensor_tensor(s["quot2"][:, :], s["ns"][:, :], s["re2"][:, :], op=ALU.mult).then_inc(tail_dve, 1)
                own("quot2")
                eng.tensor_tensor(s["root2"][:, :], s["e2"][:, :], s["quot2"][:, :], op=ALU.add).then_inc(tail_dve, 1)
                own("root2")
                eng.reciprocal(s["rn"][:, :], s["root2"][:, :]).then_inc(tail_dve, 1)
            if stage_no == 8:
                eng.wait_ge(tail_act, ab + A["exp_n"])
                eng.reciprocal(s["ren"][:, :], s["en"][:, :]).then_inc(tail_dve, 1)
                own("ren")
                eng.tensor_tensor(s["diff"][:, :], s["en"][:, :], s["ren"][:, :], op=ALU.subtract).then_inc(tail_dve, 1)
                own("diff")
                eng.scalar_tensor_tensor(out=s["F"][:, :], in0=s["diff"][:, :], scalar=0.5 / HALF_ROOT,
                                         in1=s["rn"][:, :], op0=ALU.mult, op1=ALU.mult).then_inc(tail_dve, 1)
                eng.tensor_tensor(s["hsum"][:, :], s["en"][:, :], s["ren"][:, :], op=ALU.add).then_inc(tail_dve, 1)
                own("hsum")
                eng.wait_ge(row_io[i], io_val)
                for b in range(CB):
                    eng.scalar_tensor_tensor(out=o[i][:, b, :], in0=sig[:, b, :], scalar=s["F"][:, b:b + 1],
                                             in1=x_res[i][:, b, :], op0=ALU.mult, op1=ALU.add).then_inc(tail_dve, 1)
                own("o3")
                eng.scalar_tensor_tensor(out=o[i][:, :, 0], in0=s["hsum"][:, :], scalar=0.5,
                                         in1=x_res[i][:, :, 0], op0=ALU.mult, op1=ALU.add).then_inc(tail_dve, 1)

        def tail_scalar(eng, vb, ab, acc_src, acc_sem, acc_val):
            s = small
            eng.wait_ge(acc_sem, acc_val)
            eng.activation(accS[:, :], acc_src, ACT.Copy).then_inc(tail_act, 1)
            eng.wait_ge(tail_dve, vb + V["rden"])
            for b in range(CB):
                eng.activation(E[:, b, :], Z[:, b, :], ACT.Exp, scale=s["rden"][:, b:b + 1]).then_inc(tail_act, 1)
            eng.wait_ge(tail_dve, vb + V["y3"])
            eng.activation(sq[:, :, :], y[:, :, :], ACT.Square).then_inc(tail_act, 1)
            eng.wait_ge(tail_dve, vb + V["one_q"])
            eng.activation(sp_e[:, :, :], sp[:, :, :], ACT.Ln).then_inc(tail_act, 1)
            eng.wait_ge(tail_act, ab + A["ln1"])
            eng.activation(sp_e[:, :, :], sp_e[:, :, :], ACT.Exp, scale=0.5).then_inc(tail_act, 1)
            eng.wait_ge(tail_dve, vb + V["w"])
            eng.activation(s["acosh"][:, :], s["w"][:, :], ACT.Ln, bias=1.0).then_inc(tail_act, 1)
            eng.wait_ge(tail_dve, vb + V["f"])
            for b in range(CB):
                eng.activation(sig[:, b, :], y[:, b, :], ACT.Sigmoid, scale=s["f"][:, b:b + 1]).then_inc(tail_act, 1)
            eng.wait_ge(tail_act, ab + A["s3"])
            eng.activation(sq[:, :, :], sig[:, :, :], ACT.Square).then_inc(tail_act, 1)
            eng.wait_ge(tail_dve, vb + V["ns"])
            eng.activation(s["ln2"][:, :], s["ns"][:, :], ACT.Ln).then_inc(tail_act, 1)
            eng.wait_ge(tail_act, ab + A["ln2"])
            eng.activation(s["e2"][:, :], s["ln2"][:, :], ACT.Exp, scale=0.5).then_inc(tail_act, 1)
            eng.wait_ge(tail_dve, vb + V["root2"])
            eng.activation(s["en"][:, :], s["root2"][:, :], ACT.Exp, scale=HALF_ROOT).then_inc(tail_act, 1)

        def tail_tensor(eng, vb, ab):
            eng.wait_ge(tail_act, ab + A["acc"])
            eng.wait_ge(tail_dve, vb + V["flag"])
            for b in range(CB):
                nc.tensor.matmul(Z[:, b, :], accS[:, b * P:(b + 1) * P], wa[:, :], start=True, stop=False)
                last = nc.tensor.matmul(Z[:, b, :], empty[:, b * P:(b + 1) * P], mean_row[:, :],
                                        start=False, stop=True)
            last.then_inc(tail_mm, 1)

        @block.vector
        def _(eng):
            c = col
            n = [0]

            def step(ins):
                n[0] += 1
                ins.then_inc(prep_dve, 1)

            def settle():
                eng.wait_ge(prep_dve, n[0])

            def mul(dst, a, b):
                step(eng.tensor_tensor(dst, a, b, op=ALU.mult))

            for g in range(XG):
                G = slice(g * GB, (g + 1) * GB)
                eng.wait_ge(x_in[g], 16)
                for b in range(g * GB, (g + 1) * GB):
                    step(eng.bn_stats(stats[:, b, :], z[:, b, :]))
                settle()
                step(eng.tensor_tensor(c["msum"][:, G], stats[:, G, 1], stats[:, G, 4], op=ALU.add))
                settle()
                step(eng.tensor_scalar(out=c["mean"][:, G], in0=c["msum"][:, G], scalar1=0.5, scalar2=None, op0=ALU.mult))
                settle()
                for b in range(g * GB, (g + 1) * GB):
                    ins = eng.tensor_scalar(out=z[:, b, :], in0=z[:, b, :], scalar1=c["mean"][:, b:b + 1], scalar2=0.0,
                                            op0=ALU.subtract, op1=ALU.max)
                    if b % CB == CB - 1:
                        ins.then_inc(z_done, 1)
                if g == 0:
                    eng.wait_ge(v_mm, 1)
                    eng.tensor_copy(v_sb[:, :], misc[:, 0:1]).then_inc(v_copied, 1)
                if g == 1:
                    eng.wait_ge(v_mm, 2)
                    eng.tensor_copy(wg[:, 0:1], misc[:, 1:2]).then_inc(v_copied, 1)

            step(eng.tensor_tensor(c["d"][:, :], stats[:, :, 1], stats[:, :, 4], op=ALU.subtract))
            step(eng.tensor_tensor(c["m2"][:, :], stats[:, :, 2], stats[:, :, 5], op=ALU.add))
            settle()
            mul(c["d"][:, :], c["d"][:, :], c["d"][:, :])
            settle()
            step(eng.scalar_tensor_tensor(out=c["ve"][:, :], in0=c["d"][:, :], scalar=D / 4.0, in1=c["m2"][:, :],
                                          op0=ALU.mult, op1=ALU.add))
            settle()
            step(eng.tensor_scalar(out=c["ve"][:, :], in0=c["ve"][:, :], scalar1=1.0 / D, scalar2=LN_EPS,
                                   op0=ALU.mult, op1=ALU.add))
            ve_at.append(n[0])
            eng.wait_ge(prep_act, PA["rstd0"])
            mul(c["d"][:, :], c["r0"][:, :], c["r0"][:, :])
            settle()
            mul(c["d"][:, :], c["d"][:, :], c["ve"][:, :])
            settle()
            step(eng.tensor_scalar(out=c["d"][:, :], in0=c["d"][:, :], scalar1=-0.5, scalar2=1.5,
                                   op0=ALU.mult, op1=ALU.add))
            settle()
            mul(c["rstd"][:, :], c["d"][:, :], c["r0"][:, :])
            settle()
            mul(c["u1"][:, :], z[:, :, 0], c["rstd"][:, :])
            settle()
            step(eng.tensor_scalar(out=c["u1"][:, :], in0=c["u1"][:, :], scalar1=1.0 + EPS, scalar2=-1.0,
                                   op0=ALU.max, op1=ALU.add))
            settle()
            step(eng.scalar_tensor_tensor(out=pair[:, 0, :], in0=c["u1"][:, :], scalar=2.0, in1=c["u1"][:, :],
                                          op0=ALU.add, op1=ALU.mult))
            for g in range(XG):
                G = slice(g * GB, (g + 1) * GB)
                eng.wait_ge(sqz_done, 2 * g + 2)
                step(eng.tensor_reduce(out=c["zq"][:, G], in_=sqz[:, G, 1:D], axis=AX.X, op=ALU.add))
            settle()
            mul(c["zq"][:, :], c["zq"][:, :], c["rstd"][:, :])
            settle()
            mul(c["zq"][:, :], c["zq"][:, :], c["rstd"][:, :])
            settle()
            step(eng.tensor_scalar(out=pair[:, 1, :], in0=c["zq"][:, :], scalar1=NORM2_MIN, scalar2=ROOT_SCALE,
                                   op0=ALU.max, op1=ALU.mult))
            pair_at.append(n[0])
            for g in range(XG - 1):
                G = slice(g * GB, (g + 1) * GB)
                eng.wait_ge(sqH_done, 2 * g + 2)
                step(eng.tensor_reduce(out=c["wq"][:, G], in_=sqH[:, G, 1:D], axis=AX.X, op=ALU.add))
            eng.wait_ge(prep_act, PA["pair"])
            step(eng.reciprocal(pair_r[:, :, :], pair_e[:, :, :]))
            settle()
            mul(pair_r[:, :, :], pair[:, :, :], pair_r[:, :, :])
            settle()
            step(eng.tensor_tensor(pair_r[:, :, :], pair_e[:, :, :], pair_r[:, :, :], op=ALU.add))
            settle()
            step(eng.scalar_tensor_tensor(out=c["w"][:, :], in0=pair_r[:, 0, :], scalar=0.5, in1=c["u1"][:, :],
                                          op0=ALU.mult, op1=ALU.add))
            w1_at.append(n[0])
            step(eng.reciprocal(c["rn"][:, :], pair_r[:, 1, :]))
            eng.wait_ge(sqH_done, 2 * XG)
            G = slice((XG - 1) * GB, NB)
            eng.tensor_reduce(out=c["wq"][:, G], in_=sqH[:, G, 1:D], axis=AX.X, op=ALU.add).then_inc(sqH_done, 1)
            eng.wait_ge(prep_act, PA["acosh1"])
            step(eng.scalar_tensor_tensor(out=c["r"][:, :], in0=c["acosh1"][:, :], scalar=1.0 / HALF_ROOT,
                                          in1=c["rstd"][:, :], op0=ALU.mult, op1=ALU.mult))
            settle()
            mul(c["r"][:, :], c["r"][:, :], c["rn"][:, :])
            settle()
            eng.wait_ge(sqH_done, 2 * XG + 1)
            mul(c["n2"][:, :], c["r"][:, :], c["wq"][:, :])
            settle()
            mul(c["n2"][:, :], c["n2"][:, :], c["r"][:, :])
            settle()
            step(eng.tensor_scalar(out=c["n2"][:, :], in0=c["n2"][:, :], scalar1=NORM2_MIN, scalar2=ROOT_SCALE,
                                   op0=ALU.max, op1=ALU.mult))
            n2_at.append(n[0])
            eng.wait_ge(prep_act, PA["e_n"])
            step(eng.reciprocal(c["re_n"][:, :], c["e_n"][:, :]))
            settle()
            mul(c["re_n"][:, :], c["n2"][:, :], c["re_n"][:, :])
            settle()
            step(eng.tensor_tensor(c["root_n"][:, :], c["e_n"][:, :], c["re_n"][:, :], op=ALU.add))
            rootn_at.append(n[0])
            settle()
            step(eng.reciprocal(c["rn"][:, :], c["root_n"][:, :]))
            eng.wait_ge(prep_act, PA["en"])
            step(eng.reciprocal(c["ren"][:, :], c["en"][:, :]))
            settle()
            step(eng.tensor_tensor(c["sh2"][:, :], c["en"][:, :], c["ren"][:, :], op=ALU.subtract))
            step(eng.tensor_tensor(c["ch"][:, :], c["en"][:, :], c["ren"][:, :], op=ALU.add))
            settle()
            step(eng.tensor_scalar(out=c["ch"][:, :], in0=c["ch"][:, :], scalar1=0.5, scalar2=1.0,
                                   op0=ALU.mult, op1=ALU.add))
            settle()
            step(eng.reciprocal(c["rch"][:, :], c["ch"][:, :]))
            step(eng.scalar_tensor_tensor(out=c["u"][:, :], in0=c["sh2"][:, :], scalar=0.25, in1=c["sh2"][:, :],
                                          op0=ALU.mult, op1=ALU.mult))
            settle()
            mul(c["u"][:, :], c["u"][:, :], c["rch"][:, :])
            step(eng.tensor_scalar(out=c["w"][:, :], in0=c["sh2"][:, :], scalar1=0.5, scalar2=S_EPS,
                                   op0=ALU.mult, op1=ALU.max))
            settle()
            step(eng.scalar_tensor_tensor(out=c["w"][:, :], in0=c["u"][:, :], scalar=EPS, in1=c["w"][:, :],
                                          op0=ALU.max, op1=ALU.add))
            w2_at.append(n[0])
            eng.wait_ge(prep_act, PA["acosh2"])
            step(eng.scalar_tensor_tensor(out=c["gr"][:, :], in0=c["acosh2"][:, :], scalar=1.0 / HALF_ROOT,
                                          in1=c["rn"][:, :], op0=ALU.mult, op1=ALU.mult))
            settle()
            mul(c["gr"][:, :], c["gr"][:, :], c["r"][:, :])
            settle()
            mul(c["t"][:, :], c["gr"][:, :], H[:, :, 0])
            settle()
            eng.tensor_reduce(out=tmm[:, 0:1], in_=c["t"][:, :], axis=AX.X, op=ALU.max).then_inc(tmm_done, 1)
            eng.tensor_reduce(out=tmm[:, 1:2], in_=c["t"][:, :], axis=AX.X, op=ALU.min, negate=True).then_inc(tmm_done, 1)

            def scale_rows(first, last):
                for b in range(first, last):
                    eng.tensor_scalar(out=H[:, b, 1:D], in0=H[:, b, 1:D], scalar1=c["gr"][:, b:b + 1],
                                      scalar2=None, op0=ALU.mult).then_inc(H_scaled, 1)

            eng.memset(H[:, :, 0], 1.0).then_inc(H_scaled, 1)
            scale_rows(0, 4)
            eng.wait_ge(tmmT_done, 1)
            eng.tensor_reduce(out=gmm[:, :], in_=misc[0:1, 0:2 * P].rearrange("o (a p) -> o a p", a=2),
                              axis=AX.X, op=ALU.max).then_inc(gmm_done, 1)
            scale_rows(4, 6)
            eng.wait_ge(gmm_all, 1)
            step(eng.tensor_scalar(out=shift[:, :], in0=misc[:, 256:257], scalar1=-1.0, scalar2=SHIFT,
                                   op0=ALU.mult, op1=ALU.add))
            shift_at.append(n[0])
            step(eng.tensor_copy(spread[:, :], misc[:, 257:258]))
            settle()
            step(eng.tensor_tensor(spread[:, :], misc[:, 256:257], spread[:, :], op=ALU.add))
            settle()
            eng.tensor_scalar(out=wide[:, :], in0=spread[:, :], scalar1=RANGE_LIMIT, scalar2=None,
                              op0=ALU.is_gt).then_inc(wide_done, 1)
            scale_rows(6, TJ * 2)
            eng.wait_ge(prep_act, PA["p"])
            step(eng.tensor_copy(w_bf[:, :], c["p"][:, :]))
            settle()
            step(eng.reciprocal(c["rw"][:, :], w_bf[:, :]))
            settle()
            step(eng.scalar_tensor_tensor(out=c["f"][:, :], in0=c["p"][:, :], scalar=SPLIT_SCALE, in1=c["rw"][:, :],
                                          op0=ALU.mult, op1=ALU.mult))
            settle()

            def split_rows(first, last):
                eng.wait_ge(H_scaled, last + 1)
                for b in range(first, last):
                    eng.tensor_scalar(out=hi[:, b, :], in0=H[:, b, :], scalar1=c["f"][:, b:b + 1], scalar2=None,
                                      op0=ALU.mult).then_inc(split_done, 1)
                for b in range(first, last):
                    eng.wait_ge(split_done, 2 * first + (b - first) + 1)
                    eng.scalar_tensor_tensor(out=lo[:, b, :], in0=H[:, b, :], scalar=c["f"][:, b:b + 1],
                                             in1=hi[:, b, :], op0=ALU.mult, op1=ALU.subtract).then_inc(split_done, 1)

            def mask_tile(s, k, load_no, tile_no):
                eng.wait_ge(raw_in[s], load_no)
                if tile_no is not None:
                    eng.wait_ge(mm_done, tile_no - MASKS + 1)
                for j in range(TJ):
                    b = k * TJ + j
                    ins = eng.tensor_scalar(out=mask[:, k % MASKS, j, :], in0=raw[:, s, j * CW:(j + 1) * CW],
                                            scalar1=0.0, scalar2=w_bf[:, b:b + 1], op0=ALU.is_gt, op1=ALU.mult)
                ins.then_inc(masked, 1)

            for k in range(NT):
                if k < NT - 2:
                    scale_rows((k + 2) * TJ, (k + 3) * TJ)
                split_rows(k * TJ, (k + 1) * TJ)
                mask_tile(k, k, 16, k if k >= MASKS else None)

            def chunk(cc, i, load_no):
                for k in range(NT):
                    mask_tile(i * NT + k, k, load_no, cc * NT + k)
                    args = (1 - i, (cc - 1) * NV, (cc - 1) * NA, cc - 1,
                            (cc - 1 - (1 - i)) * 16 + 16)
                    tail_vector(eng, k, *args)
                tail_vector(eng, NT, *args)

            eng.wait_ge(hsum_done, 1)
            eng.tensor_copy(hmean[:, :], misc[:, 300:301]).then_inc(hmean_done, 1)
            eng.wait_ge(mrow_mm, 1)
            eng.tensor_copy(mean_row[:, :], misc[0:1, 384:384 + P]).then_inc(mrow_done, 1)
            chunk(1, 1, 16)
            with eng.Fori(1, NC // 2) as m:
                chunk(m * 2, 0, m * 16 + 16)
                chunk(m * 2 + 1, 1, m * 16 + 16)
            for k in range(NT + 1):
                tail_vector(eng, k, 1, (NC - 1) * NV, (NC - 1) * NA, NC - 1, 16 * (NC - 1))

            eng.wait_ge(wide_done, 1)
            go = eng.value_load(wide[0:1, 0:1], min_val=0, max_val=1)
            with eng.If(go == 1):
                eng.nop().then_inc(g_free, 1)
                with eng.Fori(0, NC) as cc:
                    with eng.Fori(0, NT) as k:
                        eng.wait_ge(g_raw, cc * (16 * NT) + k * 16 + 16)
                        eng.tensor_copy(tG[:, :], c["t"][:, bass.ds(k * TJ, TJ)]).then_inc(g_step, 1)
                        eng.tensor_scalar(out=fillG, in0=rawG, scalar1=0.0, scalar2=MASK_FILL,
                                          op0=ALU.is_le, op1=ALU.mult).then_inc(g_step, 1)
                        eng.wait_ge(g_step, cc * (3 * NT) + k * 3 + 2)
                        for j in range(TJ):
                            ins = eng.tensor_scalar(out=eG[:, j, :], in0=rawG[:, j, :], scalar1=0.0,
                                                    scalar2=tG[:, j:j + 1], op0=ALU.is_gt, op1=ALU.mult)
                        ins.then_inc(g_step, 1)
                        eng.wait_ge(g_step, cc * (3 * NT) + k * 3 + 3)
                        eng.nop().then_inc(g_free, 1)
                        eng.tensor_tensor(eG, eG, fillG, op=ALU.add).then_inc(g_e, 1)
                        eng.wait_ge(g_tp, cc * NT + k + 1)
                        for b in range(CB):
                            eng.tensor_copy(sG[:, b, bass.ds(k * CW, CW)], bank[3 + b][:, :]).then_inc(g_max, 1)
                    eng.wait_ge(g_max, cc * (NT * CB + 1) + NT * CB)
                    eng.tensor_reduce(out=nmG[:, :], in_=sG, axis=AX.X, op=ALU.max, negate=True).then_inc(g_max, 1)
                    eng.wait_ge(g_exp, cc * CB + CB)
                    eng.memset(accG, 0.0).then_inc(g_acc, 1)
                    with eng.Fori(0, NB) as b:
                        eng.tensor_copy(pG, sG[:, :, bass.ds(b * P, P)]).then_inc(g_col, 1)
                        eng.tensor_copy(hG, H[:, bass.ds(b, 1), :].rearrange("p a d -> p (a d)")).then_inc(g_col, 1)
                        eng.wait_ge(g_colT, cc * NB + b + 1)
                        eng.tensor_copy(pTG, bank[3][:, :]).then_inc(g_pT, 1)
                        eng.wait_ge(g_mm, cc * NB + b + 1)
                        eng.wait_ge(g_acc, cc * (NB + 1) + b + 1)
                        eng.tensor_tensor(accG, bank[4][:, :], accG, op=ALU.add).then_inc(g_acc, 1)
                    for k in range(NT + 1):
                        tail_vector(eng, k, 0, cc * NV + NV * NC, cc * NA + NA * NC, cc + NC,
                                    cc * 32 + 16 * NC + 16)

        @block.scalar
        def _(eng):
            c = col
            eng.wait_ge(zero_done, 3)
            eng.dma_start(waT[:, :], w_att_t).then_inc(const_in, 16)
            eng.dma_start(a2s[:, :], a2).then_inc(const_in, 16)
            eng.dma_start(wgT[1:P, 1:P], w_gcn_t).then_inc(const_in, 16)
            eng.dma_start(wg[1:P, 1:P], w_gcn).then_inc(const_in, 16)
            eng.dma_start(wa[1:P, 1:P], w_att[1:P, 1:P]).then_inc(att_in, 16)

            def step(ins, name):
                assert PA[name] == len(seen) + 1
                seen.append(name)
                ins.then_inc(prep_act, 1)

            def own(name):
                eng.wait_ge(prep_act, PA[name])

            def copy_H(u):
                B = slice(u * CB, (u + 1) * CB)
                eng.wait_ge(zw_done, u + 1)
                eng.activation(H[:, B, :], zw_ring[u % 3][:, :].rearrange("p (b d) -> p b d", d=D),
                               ACT.Copy).then_inc(H_done, 1)

            def square_H(u):
                B = slice(u * CB, (u + 1) * CB)
                eng.wait_ge(H_done, u + 1)
                eng.activation(sqH[:, B, :], H[:, B, :], ACT.Square).then_inc(sqH_done, 1)

            U = NB // CB
            for u in range(U):
                B = slice(u * CB, (u + 1) * CB)
                eng.wait_ge(tp_done, u + 1)
                eng.activation(zT[:, B, :], tp_ring[u % 4][:, :].rearrange("p (b d) -> p b d", d=D),
                               ACT.Copy).then_inc(zT_done, 1)
                eng.wait_ge(z_done, u + 1)
                eng.activation(sqz[:, B, :], z[:, B, :], ACT.Square).then_inc(sqz_done, 1)
                if u >= 1:
                    copy_H(u - 1)
                if u >= 2:
                    square_H(u - 2)
                if u == U - 2:
                    eng.wait_ge(prep_dve, ve_at[0])
                    step(eng.activation(c["lv"][:, :], c["ve"][:, :], ACT.Ln), "ln_ve")
                    own("ln_ve")
                    step(eng.activation(c["r0"][:, :], c["lv"][:, :], ACT.Exp, scale=-0.5), "rstd0")
            copy_H(U - 1)
            square_H(U - 2)
            square_H(U - 1)
            eng.wait_ge(prep_dve, pair_at[0])
            step(eng.activation(pair_e[:, :, :], pair[:, :, :], ACT.Ln), "ln_pair")
            own("ln_pair")
            step(eng.activation(pair_e[:, :, :], pair_e[:, :, :], ACT.Exp, scale=0.5), "pair")
            eng.wait_ge(prep_dve, w1_at[0])
            step(eng.activation(c["acosh1"][:, :], c["w"][:, :], ACT.Ln, bias=1.0), "acosh1")
            eng.wait_ge(prep_dve, n2_at[0])
            step(eng.activation(c["ln_n"][:, :], c["n2"][:, :], ACT.Ln), "ln_n")
            own("ln_n")
            step(eng.activation(c["e_n"][:, :], c["ln_n"][:, :], ACT.Exp, scale=0.5), "e_n")
            eng.wait_ge(prep_dve, rootn_at[0])
            step(eng.activation(c["en"][:, :], c["root_n"][:, :], ACT.Exp, scale=HALF_ROOT), "en")
            eng.wait_ge(prep_dve, w2_at[0])
            step(eng.activation(c["acosh2"][:, :], c["w"][:, :], ACT.Ln, bias=1.0), "acosh2")
            eng.wait_ge(prep_dve, shift_at[0])
            step(eng.activation(c["p"][:, :], c["t"][:, :], ACT.Exp, bias=shift[:, :]), "p")

            tail_scalar(eng, 0, 0, acc[0][:, :], mm_done, NT)
            with eng.Fori(1, NC // 2) as m:
                for i in (1, 0):
                    cc = m * 2 - i
                    tail_scalar(eng, cc * NV, cc * NA, acc[i][:, :], mm_done, cc * NT + NT)
            tail_scalar(eng, (NC - 1) * NV, (NC - 1) * NA, acc[1][:, :], mm_done, NC * NT)

            eng.wait_ge(wide_done, 1)
            go = eng.value_load(wide[0:1, 0:1], min_val=0, max_val=1)
            with eng.If(go == 1):
                with eng.Fori(0, NC) as cc:
                    eng.wait_ge(g_max, cc * (NT * CB + 1) + NT * CB + 1)
                    for b in range(CB):
                        eng.activation(sG[:, b, :], sG[:, b, :], ACT.Exp, bias=nmG[:, b:b + 1]).then_inc(g_exp, 1)
                    tail_scalar(eng, cc * NV + NV * NC, cc * NA + NA * NC, accG, g_acc, cc * (NB + 1) + NB + 1)

        @block.tensor
        def _(eng):
            eng.wait_ge(const_in, 64)
            nc.tensor.matmul(misc[:, 0:1], waT[:, :], a2s[:, :], start=True, stop=True).then_inc(v_mm, 1)
            eng.wait_ge(ident_done, 2)

            def transpose_z(u):
                eng.wait_ge(z_done, u + 1)
                if u >= 4:
                    eng.wait_ge(zT_done, u - 3)
                for b in range(CB):
                    ins = nc.tensor.transpose(tp_ring[u % 4][:, b * P:(b + 1) * P], z[:, u * CB + b, :], ident[:, :])
                ins.then_inc(tp_done, 1)

            def product(u):
                eng.wait_ge(zT_done, u + 1)
                if u >= 3:
                    eng.wait_ge(H_done, u - 2)
                for b in range(CB):
                    ins = nc.tensor.matmul(zw_ring[u % 3][:, b * P:(b + 1) * P], zT[:, u * CB + b, :], wg[:, :],
                                           start=True, stop=True)
                ins.then_inc(zw_done, 1)

            U = NB // CB
            transpose_z(0)
            transpose_z(1)
            eng.wait_ge(v_copied, 1)
            nc.tensor.matmul(misc[:, 1:2], wgT[:, :], v_sb[:, :], start=True, stop=True).then_inc(v_mm, 1)
            eng.wait_ge(v_copied, 2)
            for u in range(2, U + 2):
                if u < U:
                    transpose_z(u)
                product(u - 2)

            eng.wait_ge(tmm_done, 2)
            nc.tensor.transpose(misc[0:1, 0:P], tmm[:, 0:1], ident[:, :])
            nc.tensor.transpose(misc[0:1, P:2 * P], tmm[:, 1:2], ident[:, :]).then_inc(tmmT_done, 1)
            eng.wait_ge(gmm_done, 1)
            eng.wait_ge(const_done, 3)
            nc.tensor.matmul(misc[:, 256:258], ones_row[:, :], gmm[:, :], start=True, stop=True).then_inc(gmm_all, 1)
            eng.wait_ge(wide_done, 1)

            def tile(a, k, tile_no):
                eng.wait_ge(masked, tile_no + 1)
                for j in range(TJ):
                    b = k * TJ + j
                    nc.tensor.matmul(a[:, :], hi[:, b, :], mask[:, k % MASKS, j, :],
                                     start=(b == 0), stop=False)
                    ins = nc.tensor.matmul(a[:, :], lo[:, b, :], mask[:, k % MASKS, j, :],
                                           start=False, stop=(b == NB - 1))
                ins.then_inc(mm_done, 1)

            eng.wait_ge(const_done, 3)
            for k in range(NT):
                tile(acc[0], k, k)
                for b in range(k * TJ, (k + 1) * TJ):
                    ins = nc.tensor.matmul(misc[:, 300:301], H[:, b, :], inv_n[:, :],
                                           start=(b == 0), stop=(b == NB - 1))
            ins.then_inc(hsum_done, 1)
            eng.wait_ge(hmean_done, 1)
            eng.wait_ge(att_in, 16)
            nc.tensor.matmul(misc[0:1, 384:384 + P], hmean[:, :], wa[:, :], start=True, stop=True).then_inc(mrow_mm, 1)
            eng.wait_ge(mrow_done, 1)

            def chunk(cc, i):
                for k in range(NT):
                    tile(acc[i], k, cc * NT + k)
                    if k == 0:
                        tail_tensor(eng, (cc - 1) * NV, (cc - 1) * NA)

            chunk(1, 1)
            with eng.Fori(1, NC // 2) as m:
                chunk(m * 2, 0)
                chunk(m * 2 + 1, 1)
            tail_tensor(eng, (NC - 1) * NV, (NC - 1) * NA)

            go = eng.value_load(wide[0:1, 0:1], min_val=0, max_val=1)
            with eng.If(go == 1):
                with eng.Fori(0, NC) as cc:
                    with eng.Fori(0, NT) as k:
                        eng.wait_ge(g_e, cc * NT + k + 1)
                        for b in range(CB):
                            for j in range(TJ):
                                ins = nc.tensor.transpose(bank[3 + b][:, j * P:(j + 1) * P],
                                                          eG[:, j, b * P:(b + 1) * P], ident[:, :])
                        ins.then_inc(g_tp, 1)
                    with eng.Fori(0, NB) as b:
                        eng.wait_ge(g_col, cc * (2 * NB) + b * 2 + 2)
                        for q in range(CB):
                            ins = nc.tensor.transpose(bank[3][:, q * P:(q + 1) * P], pG[:, q, :], ident[:, :])
                        ins.then_inc(g_colT, 1)
                        eng.wait_ge(g_pT, cc * NB + b + 1)
                        nc.tensor.matmul(bank[4][:, :], hG, pTG, start=True, stop=True).then_inc(g_mm, 1)
                    tail_tensor(eng, cc * NV + NV * NC, cc * NA + NA * NC)


PA = {n: i + 1 for i, n in enumerate(
    ["ln_ve", "rstd0", "ln_pair", "pair", "acosh1", "ln_n", "e_n", "en", "acosh2", "p"])}
seen, ve_at, pair_at, w1_at, n2_at, rootn_at, w2_at, shift_at = ([] for _ in range(8))

_INS = ["x", "adj_t", "w_gcn", "w_gcn_t", "w_att", "w_att_t", "a2"]


def kernel(**inputs):
    import numpy as _np
    import concourse.bacc as _bacc
    from concourse import mybir as _mybir
    from concourse.bass_utils import run_bass_kernel_spmd as _run

    for marks in (seen, ve_at, pair_at, w1_at, n2_at, rootn_at, w2_at, shift_at):
        marks.clear()
    adj = _np.asarray(inputs["adj"])
    w_gcn = _np.asarray(inputs["L0_gnn_W_gcn"])
    w_att = _np.asarray(inputs["L0_gnn_W_att"])
    tiles = adj.reshape(NC, P, CB, P, NT, TJ).transpose(0, 4, 3, 5, 2, 1)
    host = {
        "x": inputs["x"],
        "adj_t": _np.ascontiguousarray(tiles).reshape(NC, NT, P, TJ * CW),
        "w_gcn": w_gcn, "w_gcn_t": w_gcn.T, "w_att": w_att, "w_att_t": w_att.T,
        "a2": _np.asarray(inputs["L0_gnn_a_att"])[D:],
    }
    nc = _bacc.Bacc("TRN2", target_bir_lowering=False, num_devices=1)
    arrays, args = {}, []
    for name in _INS:
        a = _np.ascontiguousarray(host[name])
        arrays[f"in_{name}_dram"] = a
        args.append(nc.dram_tensor(f"in_{name}_dram", a.shape, _mybir.dt.from_np(a.dtype), kind="ExternalInput").ap())
    args.append(nc.dram_tensor("out_0_dram", (N, D), _mybir.dt.float32, kind="ExternalOutput").ap())
    build(nc, *args)
    r = _run(nc, [arrays], core_ids=[0])
    return r.results[0]["out_0_dram"]
```

```python
import math
from contextlib import ExitStack

import concourse.bass as bass
from concourse import mybir

N, D = 4096, 128
P = 128
NB = N // P
HALF = 512
TILE = 2048
HT = TILE // 2
WIDE_B, SLIM_B = 8, 4
WIDE_N, SLIM_N = 3, 2
CHUNKS = WIDE_N + SLIM_N
WT = NB // 2
ST = NB // 4
TILES = WIDE_N * WT + SLIM_N * ST
SLOTS = WT
MASKS = 4
UNITS = 2 * WIDE_N + SLIM_N
QB = HALF // P
QN = NB // QB
XG = 4
GB = NB // XG
LN_EPS = 1e-5
EPS = 2.0 ** -23
S_EPS = math.sqrt(EPS * (EPS + 2.0))
NORM2_MIN = 1e-30
ROOT_SCALE = 2.0 ** 40
HALF_ROOT = 2.0 ** -21
MASK_FILL = -9000000000000000.0
SHIFT = 60.0
RANGE_LIMIT = 125.0
SPLIT_SCALE = 512.0

V = {n: i + 1 for i, n in enumerate(
    ["flag", "rden", "em", "y", "q", "lift", "one_q", "re", "quot", "root", "xp", "rxp", "u", "m",
     "w", "ryn", "f", "ssq", "ns", "re2", "quot2", "root2", "rn", "ren", "diff", "F", "hsum", "o",
     "col0"])}
A = {n: i + 1 for i, n in enumerate(
    ["acc", "e", "sq_y", "ln1", "exp1", "ln_w", "sig", "sq_s", "ln2", "exp2", "exp_n"])}
NV, NA = len(V), len(A)
WIDE_STAGES = {0: [0], 3: [1], 5: [2], 7: [3], 8: [4], 9: [5], 13: [6], 14: [7], 15: [8]}
SLIM_STAGES = {0: [0], 1: [1], 2: [2], 3: [3], 4: [4], 5: [5], 6: [6], 7: [7, 8]}


def build(nc, x, adj_t, w_gcn, w_gcn_t, w_att, w_att_t, a2, out):
    f32, bf16, f16, i32 = mybir.dt.float32, mybir.dt.bfloat16, mybir.dt.float16, mybir.dt.int32
    ALU, ACT, AX = mybir.AluOpType, mybir.ActivationFunctionType, mybir.AxisListType

    x_blocks = x.rearrange("(p b) d -> p b d", b=NB)
    out_blocks = out.rearrange("(p b) d -> p b d", b=NB)
    halves = adj_t.rearrange("t p (h n) -> t h p n", h=2)

    with ExitStack() as ctx:
        def sb(name, shape, dt):
            return ctx.enter_context(nc.sbuf_tensor(name, shape, dt))

        def sem(name):
            return ctx.enter_context(nc.semaphore(name))

        raw = sb("raw", [P, SLOTS, TILE], i32)
        xs = sb("xs", [P, NB, D], f32)
        H = sb("H", [P, NB, D], f32)
        split = sb("split", [P, 2, NB, D], f16)
        hi, lo = split[:, 0], split[:, 1]
        masks = sb("masks", [P, MASKS, TILE], bf16)
        mask = masks[:, :, :].rearrange("p s (h j i) -> p s h j i", h=2, j=2)
        rawv = raw[:, :, :].rearrange("p s (h j i) -> p s h j i", h=2, j=2)

        arena = masks[:, 2:MASKS, :].rearrange("p s n -> p (s n)").bitcast(f32)
        used = [0]

        def prep(width):
            used[0] += width
            return arena[:, used[0] - width:used[0]]

        def raw_f32(first, slots):
            return raw[:, first:first + slots, :].rearrange("p s n -> p (s n)").bitcast(f32)

        z = raw_f32(SLOTS - 6, 2).rearrange("p (b d) -> p b d", d=D)
        sqz = raw_f32(SLOTS - 4, 2).rearrange("p (b d) -> p b d", d=D)
        sqH = raw_f32(SLOTS - 2, 2).rearrange("p (b d) -> p b d", d=D)
        zT = split[:, :, :, :].rearrange("p a b d -> p (a b d)").bitcast(f32).rearrange("p (b d) -> p b d", d=D)

        accS = sb("accS", [P, WIDE_B * P], f32)
        sig = accS[:, :].rearrange("p (b d) -> p b d", d=D)
        E = sb("E", [P, WIDE_B, D], f32)
        sq = E
        empty = E[0:1, :, :].rearrange("o b d -> o (b d)")
        y = sb("y", [P, WIDE_B, D], f32)

        ident = sb("ident", [P, P], f32)
        wg = prep(P)
        wgT = prep(P)
        wa = sb("wa", [P, P], f32)
        waT = prep(P)
        a2s = prep(1)
        v_sb = prep(1)
        ones_row = sb("ones_row", [1, P], f32)
        inv_n = sb("inv_n", [P, 1], f32)
        hmean = sb("hmean", [P, 1], f32)
        mean_row = sb("mean_row", [1, P], f32)
        stats = prep(NB * 6).rearrange("p (b n) -> p b n", n=6)
        col = {n: prep(NB) for n in
               ["msum", "mean", "d", "m2", "ve", "lv", "r0", "rstd", "u1", "zq", "acosh1", "r",
                "wq", "n2", "dd", "ln_n", "e_n", "re_n", "root_n", "en", "ren", "sh2", "ch", "rch",
                "u", "w", "acosh2", "rn", "rw"]}
        col |= {n: sb("c_" + n, [P, NB], f32) for n in ["gr", "t", "p", "f"]}
        pair = prep(2 * NB).rearrange("p (a b) -> p a b", a=2)
        pair_e = prep(2 * NB).rearrange("p (a b) -> p a b", a=2)
        pair_r = prep(2 * NB).rearrange("p (a b) -> p a b", a=2)
        w_bf = sb("w_bf", [P, NB], bf16)
        tmm = prep(2)
        gmm = sb("gmm", [1, 2], f32)
        shift = prep(1)
        spread = prep(1)
        wide = sb("wide", [P, 1], i32)
        small = {n: sb("s_" + n, [P, WIDE_B], f32) for n in
                 ["rden", "q", "xp", "rxp", "u", "m", "w", "acosh", "ryn", "f", "ssq", "ns",
                  "ln2", "e2", "re2", "quot2", "root2", "rn", "en", "ren", "diff", "F", "hsum"]}
        sp = sb("sp", [P, 2, WIDE_B], f32)
        sp_e = sb("sp_e", [P, 2, WIDE_B], f32)
        sp_r = sb("sp_r", [P, 2, WIDE_B], f32)
        sp_s = sb("sp_s", [P, 2, WIDE_B], f32)
        rawG = raw[:, 0, 0:HT]
        eG = raw_f32(1, 1)[:, 0:HT].rearrange("p (j i) -> p j i", j=2)
        fillG = raw_f32(2, 1)[:, 0:HT]
        mixG = raw_f32(3, 1)
        pG = mixG[:, 0:HALF].rearrange("p (b j) -> p b j", b=SLIM_B)
        pTG = mixG[:, HALF:2 * HALF]
        accG = mixG[:, 2 * HALF:3 * HALF]
        hG = mixG[:, 3 * HALF:3 * HALF + D]
        sG = raw_f32(8, 8).rearrange("p (b j) -> p b j", b=SLIM_B)
        tG = sb("tG", [P, 2], f32)
        nmG = sb("nmG", [P, SLIM_B], f32)

        def psum(name, shape):
            return ctx.enter_context(nc.psum_tensor(name, shape, f32))

        acc_wide = psum("acc_wide", [P, 2, HALF])
        Z = psum("Z", [P, WIDE_B, D])
        acc_slim = [psum(f"acc_slim{i}", [P, HALF]) for i in range(2)]
        spare = psum("spare", [P, HALF])
        misc = psum("misc", [P, HALF])
        Zflat = Z[:, :, :].rearrange("p b d -> p (b d)")
        tp_ring = [acc_wide[:, 0, :], acc_wide[:, 1, :], Zflat[:, 0:HALF], Zflat[:, HALF:2 * HALF]]
        zw_ring = [acc_slim[0][:, :], acc_slim[1][:, :], spare[:, :]]
        tpG = [acc_wide[:, 0, :], acc_wide[:, 1, :], acc_slim[0][:, :], acc_slim[1][:, :]]

        x_in = [sem(f"x_in{g}") for g in range(XG)]
        raw_in = [sem(f"raw_in{s}") for s in range(SLOTS)]
        stored = sem("stored")
        x_again = sem("x_again")
        const_in = sem("const_in")
        att_in = sem("att_in")
        const_done = sem("const_done")
        zero_done = sem("zero_done")
        ident_done = sem("ident_done")
        prep_dve = sem("prep_dve")
        prep_act = sem("prep_act")
        variance_ready = sem("variance_ready")
        roots_ready = sem("roots_ready")
        acosh1_ready = sem("acosh1_ready")
        n2_ready = sem("n2_ready")
        root_n_ready = sem("root_n_ready")
        acosh2_ready = sem("acosh2_ready")
        gr_ready = sem("gr_ready")
        shift_ready = sem("shift_ready")
        f_ready = sem("f_ready")
        hi_done = sem("hi_done")
        v_mm = sem("v_mm")
        v_copied = sem("v_copied")
        tp_done = sem("tp_done")
        zT_done = sem("zT_done")
        zw_done = sem("zw_done")
        H_done = sem("H_done")
        sqz_done = sem("sqz_done")
        sqH_done = sem("sqH_done")
        z_done = sem("z_done")
        H_scaled = sem("H_scaled")
        tmm_done = sem("tmm_done")
        tmmT_done = sem("tmmT_done")
        gmm_done = sem("gmm_done")
        gmm_all = sem("gmm_all")
        ones_done = sem("ones_done")
        wide_done = sem("wide_done")
        masked = sem("masked")
        mm_done = sem("mm_done")
        hsum_done = sem("hsum_done")
        hmean_done = sem("hmean_done")
        mrow_mm = sem("mrow_mm")
        mrow_done = sem("mrow_done")
        tail_dve = sem("tail_dve")
        tail_act = sem("tail_act")
        tail_mm = sem("tail_mm")
        g_raw = sem("g_raw")
        g_free = sem("g_free")
        g_step = sem("g_step")
        g_e = sem("g_e")
        g_tp = sem("g_tp")
        g_max = sem("g_max")
        g_exp = sem("g_exp")
        g_col = sem("g_col")
        g_colT = sem("g_colT")
        g_pT = sem("g_pT")
        g_mm = sem("g_mm")
        g_acc = sem("g_acc")

        block = ctx.enter_context(nc.Block())

        @block.sync
        def _(eng):
            for g in range(XG):
                G = slice(g * GB, (g + 1) * GB)
                eng.dma_start(xs[:, G, :], x_blocks[:, G, :]).then_inc(x_in[g], 16)

            def load(tile, s):
                eng.dma_start(raw[:, s, :], adj_t[tile]).then_inc(raw_in[s], 16)

            def store(chunk, first, blocks):
                eng.wait_ge(tail_dve, NV * (chunk + 1))
                B = slice(first, first + blocks)
                eng.dma_start(out_blocks[:, B, :], xs[:, B, :]).then_inc(stored, 16)

            for s in range(SLOTS - 6):
                load(s, s)
            eng.wait_ge(tp_done, QN)
            eng.wait_ge(roots_ready, 1)
            for s in range(SLOTS - 6, SLOTS - 2):
                load(s, s)
            eng.wait_ge(sqH_done, QN + 1)
            for s in range(SLOTS - 2, SLOTS):
                load(s, s)
            with eng.Fori(1, WIDE_N) as c:
                for k in range(WT):
                    eng.wait_ge(masked, c * WT - WT + k + 1)
                    load(c * WT + k, k)
            for s in range(SLOTS):
                tile = WIDE_N * WT + s
                eng.wait_ge(masked, tile - SLOTS + 1)
                load(tile, s)
                if s == 0:
                    store(0, 0, WIDE_B)
            for c in range(1, WIDE_N):
                store(c, c * WIDE_B, WIDE_B)
            for c in range(SLIM_N):
                store(WIDE_N + c, WIDE_N * WIDE_B + c * SLIM_B, SLIM_B)
            eng.wait_ge(stored, 16 * CHUNKS)

            eng.wait_ge(wide_done, 1)
            go = eng.value_load(wide[0:1, 0:1], min_val=0, max_val=1)
            with eng.If(go == 1):
                eng.dma_start(xs[:, :, :], x_blocks).then_inc(x_again, 16)

                def unit(u, first, sides):
                    n = len(sides)
                    with eng.Fori(0, WT // n) as k:
                        for i, side in enumerate(sides):
                            eng.wait_ge(g_free, u * WT + k * n + (i + 1))
                            eng.dma_start(rawG, halves[first + k, side]).then_inc(g_raw, 16)
                    eng.wait_ge(tail_dve, u * NV + NV * (CHUNKS + 1))
                    eng.dma_start(out_blocks[:, bass.ds(u * SLIM_B, SLIM_B), :],
                                  xs[:, bass.ds(u * SLIM_B, SLIM_B), :]).then_inc(stored, 16)

                with eng.Fori(0, WIDE_N) as c:
                    for h in range(2):
                        unit(c * 2 + h, c * WT, [h])
                with eng.Fori(0, SLIM_N) as c:
                    unit(c + 2 * WIDE_N, c * ST + WIDE_N * WT, [0, 1])
                eng.wait_ge(stored, 16 * (CHUNKS + UNITS))

        @block.gpsimd
        def _(eng):
            eng.memset(ident[:, :], 0.0).then_inc(ident_done, 1)
            eng.memset(wg[:, :], 0.0).then_inc(zero_done, 1)
            eng.memset(wgT[:, :], 0.0).then_inc(zero_done, 1)
            eng.memset(wa[:, :], 0.0).then_inc(zero_done, 1)
            eng.wait_ge(ident_done, 1)
            eng.affine_select(out=ident[:, :], in_=ident[:, :], compare_op=ALU.not_equal, fill=1.0,
                              base=0, pattern=[[-1, P]], channel_multiplier=1).then_inc(ident_done, 1)
            eng.memset(ones_row[:, :], 1.0).then_inc(const_done, 1)
            eng.memset(inv_n[:, :], 1.0 / N).then_inc(const_done, 1)
            eng.wait_ge(zero_done, 3)
            eng.memset(wa[0:1, 0:1], 1.0).then_inc(const_done, 1)

        def tail_vector(eng, stages, n, block0, c, extra=0):
            s = {k: v[:, 0:n] for k, v in small.items()}
            vb, ab = c * NV + extra * NV, c * NA + extra * NA

            def own(name):
                eng.wait_ge(tail_dve, vb + V[name])

            def step(ins):
                ins.then_inc(tail_dve, 1)

            if 0 in stages:
                eng.wait_ge(tail_act, ab + A["acc"])
                step(eng.tensor_scalar(out=empty[:, 0:n * P], in0=accS[0:1, 0:n * P], scalar1=0.0,
                                       scalar2=None, op0=ALU.is_equal))
            if 1 in stages:
                eng.wait_ge(tail_mm, c + extra + 1)
                step(eng.reciprocal(s["rden"], Z[:, 0:n, 0]))
            if 2 in stages:
                eng.wait_ge(tail_act, ab + A["e"])
                step(eng.tensor_scalar(out=E[:, 0:n, :], in0=E[:, 0:n, :], scalar1=1.0, scalar2=-1.0,
                                       op0=ALU.min, op1=ALU.add))
                own("em")
                for b in range(n):
                    ins = eng.scalar_tensor_tensor(out=y[:, b, :], in0=Z[:, b, :], scalar=s["rden"][:, b:b + 1],
                                                   in1=E[:, b, :], op0=ALU.mult, op1=ALU.max)
                step(ins)
            if 3 in stages:
                eng.wait_ge(tail_act, ab + A["sq_y"])
                step(eng.tensor_reduce(out=s["q"], in_=sq[:, 0:n, 1:D], axis=AX.X, op=ALU.add))
                own("q")
                step(eng.tensor_scalar(out=sp[:, 0, 0:n], in0=s["q"], scalar1=NORM2_MIN, scalar2=ROOT_SCALE,
                                       op0=ALU.max, op1=ALU.mult))
                step(eng.tensor_scalar(out=sp[:, 1, 0:n], in0=s["q"], scalar1=1.0, scalar2=None, op0=ALU.add))
            if 4 in stages:
                eng.wait_ge(tail_act, ab + A["exp1"])
                step(eng.reciprocal(sp_r[:, :, 0:n], sp_e[:, :, 0:n]))
                own("re")
                step(eng.tensor_tensor(sp_r[:, :, 0:n], sp[:, :, 0:n], sp_r[:, :, 0:n], op=ALU.mult))
                own("quot")
                step(eng.tensor_tensor(sp_s[:, :, 0:n], sp_e[:, :, 0:n], sp_r[:, :, 0:n], op=ALU.add))
                own("root")
                step(eng.tensor_scalar(out=s["xp"], in0=sp_s[:, 1, 0:n], scalar1=0.5, scalar2=1.0,
                                       op0=ALU.mult, op1=ALU.add))
                own("xp")
                step(eng.reciprocal(s["rxp"], s["xp"]))
                own("rxp")
                step(eng.tensor_tensor(s["u"], s["q"], s["rxp"], op=ALU.mult))
                step(eng.tensor_scalar(out=s["m"], in0=sp_s[:, 0, 0:n], scalar1=HALF_ROOT, scalar2=S_EPS,
                                       op0=ALU.mult, op1=ALU.max))
                own("m")
                step(eng.scalar_tensor_tensor(out=s["w"], in0=s["u"], scalar=EPS, in1=s["m"],
                                              op0=ALU.max, op1=ALU.add))
                step(eng.reciprocal(s["ryn"], sp_s[:, 0, 0:n]))
            if 5 in stages:
                eng.wait_ge(tail_act, ab + A["ln_w"])
                own("ryn")
                step(eng.scalar_tensor_tensor(out=s["f"], in0=s["acosh"], scalar=1.0 / HALF_ROOT,
                                              in1=s["ryn"], op0=ALU.mult, op1=ALU.mult))
            if 6 in stages:
                eng.wait_ge(tail_act, ab + A["sq_s"])
                step(eng.tensor_reduce(out=s["ssq"], in_=sq[:, 0:n, 1:D], axis=AX.X, op=ALU.add))
                own("ssq")
                step(eng.tensor_scalar(out=s["ns"], in0=s["ssq"], scalar1=NORM2_MIN, scalar2=ROOT_SCALE,
                                       op0=ALU.max, op1=ALU.mult))
            if 7 in stages:
                eng.wait_ge(tail_act, ab + A["exp2"])
                step(eng.reciprocal(s["re2"], s["e2"]))
                own("re2")
                step(eng.tensor_tensor(s["quot2"], s["ns"], s["re2"], op=ALU.mult))
                own("quot2")
                step(eng.tensor_tensor(s["root2"], s["e2"], s["quot2"], op=ALU.add))
                own("root2")
                step(eng.reciprocal(s["rn"], s["root2"]))
            if 8 in stages:
                eng.wait_ge(tail_act, ab + A["exp_n"])
                step(eng.reciprocal(s["ren"], s["en"]))
                own("ren")
                step(eng.tensor_tensor(s["diff"], s["en"], s["ren"], op=ALU.subtract))
                own("diff")
                step(eng.scalar_tensor_tensor(out=s["F"], in0=s["diff"], scalar=0.5 / HALF_ROOT, in1=s["rn"],
                                              op0=ALU.mult, op1=ALU.mult))
                step(eng.tensor_tensor(s["hsum"], s["en"], s["ren"], op=ALU.add))
                own("hsum")
                rows = xs[:, bass.ds(block0, n), :]
                if extra:
                    eng.wait_ge(x_again, 16)
                for b in range(n):
                    ins = eng.scalar_tensor_tensor(out=rows[:, b, 1:D], in0=sig[:, b, 1:D], scalar=s["F"][:, b:b + 1],
                                                   in1=rows[:, b, 1:D], op0=ALU.mult, op1=ALU.add)
                step(ins)
                step(eng.scalar_tensor_tensor(out=rows[:, :, 0], in0=s["hsum"], scalar=0.5, in1=rows[:, :, 0],
                                              op0=ALU.mult, op1=ALU.add))

        def tail_scalar(eng, n, acc_src, acc_sem, acc_val, c, extra=0):
            s = {k: v[:, 0:n] for k, v in small.items()}
            vb, ab = c * NV + extra * NV, c * NA + extra * NA

            def step(ins):
                ins.then_inc(tail_act, 1)

            if extra or not isinstance(c, int) or c > 0:
                eng.wait_ge(tail_dve, vb)
            eng.wait_ge(acc_sem, acc_val)
            step(eng.activation(accS[:, 0:n * P], acc_src, ACT.Copy))
            eng.wait_ge(tail_dve, vb + V["rden"])
            for b in range(n):
                ins = eng.activation(E[:, b, :], Z[:, b, :], ACT.Exp, scale=s["rden"][:, b:b + 1])
            step(ins)
            eng.wait_ge(tail_dve, vb + V["y"])
            step(eng.activation(sq[:, 0:n, :], y[:, 0:n, :], ACT.Square))
            eng.wait_ge(tail_dve, vb + V["one_q"])
            step(eng.activation(sp_e[:, :, 0:n], sp[:, :, 0:n], ACT.Ln))
            eng.wait_ge(tail_act, ab + A["ln1"])
            step(eng.activation(sp_e[:, :, 0:n], sp_e[:, :, 0:n], ACT.Exp, scale=0.5))
            eng.wait_ge(tail_dve, vb + V["w"])
            step(eng.activation(s["acosh"], s["w"], ACT.Ln, bias=1.0))
            eng.wait_ge(tail_dve, vb + V["f"])
            for b in range(n):
                ins = eng.activation(sig[:, b, :], y[:, b, :], ACT.Sigmoid, scale=s["f"][:, b:b + 1])
            step(ins)
            eng.wait_ge(tail_act, ab + A["sig"])
            step(eng.activation(sq[:, 0:n, :], sig[:, 0:n, :], ACT.Square))
            eng.preload_act_table_set("natural_log_exp_and_others")
            eng.wait_ge(tail_dve, vb + V["ns"])
            step(eng.activation(s["ln2"], s["ns"], ACT.Ln))
            eng.wait_ge(tail_act, ab + A["ln2"])
            step(eng.activation(s["e2"], s["ln2"], ACT.Exp, scale=0.5))
            eng.wait_ge(tail_dve, vb + V["root2"])
            step(eng.activation(s["en"], s["root2"], ACT.Exp, scale=HALF_ROOT))

        def tail_tensor(eng, n, c, extra=0):
            eng.wait_ge(tail_act, c * NA + (extra * NA + A["acc"]))
            eng.wait_ge(tail_dve, c * NV + (extra * NV + V["flag"]))
            for b in range(n):
                nc.tensor.matmul(Z[:, b, :], accS[:, b * P:(b + 1) * P], wa[:, :], start=True, stop=False)
                last = nc.tensor.matmul(Z[:, b, :], empty[:, b * P:(b + 1) * P], mean_row[:, :],
                                        start=False, stop=True)
            last.then_inc(tail_mm, 1)

        @block.vector
        def _(eng):
            c = col
            n = [0]
            last = [prep_dve, 0]

            def step(ins, signal=None):
                n[0] += signal is None
                last[:] = [signal, 1] if signal is not None else [prep_dve, n[0]]
                ins.then_inc(last[0], 1)

            def settle():
                eng.wait_ge(last[0], last[1])

            def mul(dst, a, b):
                step(eng.tensor_tensor(dst, a, b, op=ALU.mult))

            for g in range(XG):
                G = slice(g * GB, (g + 1) * GB)
                eng.wait_ge(x_in[g], 16)
                for b in range(g * GB, (g + 1) * GB):
                    step(eng.bn_stats(stats[:, b, :], xs[:, b, :]))
                settle()
                step(eng.tensor_tensor(c["msum"][:, G], stats[:, G, 1], stats[:, G, 4], op=ALU.add))
                settle()
                step(eng.tensor_scalar(out=c["mean"][:, G], in0=c["msum"][:, G], scalar1=0.5, scalar2=None, op0=ALU.mult))
                settle()
                for b in range(g * GB, (g + 1) * GB):
                    ins = eng.tensor_scalar(out=z[:, b, :], in0=xs[:, b, :], scalar1=c["mean"][:, b:b + 1], scalar2=0.0,
                                            op0=ALU.subtract, op1=ALU.max)
                    if b % QB == QB - 1:
                        ins.then_inc(z_done, 1)
                if g == 0:
                    eng.wait_ge(v_mm, 1)
                    eng.tensor_copy(v_sb[:, :], misc[:, 0:1]).then_inc(v_copied, 1)
                if g == 1:
                    eng.wait_ge(v_mm, 2)
                    eng.tensor_copy(wg[:, 0:1], misc[:, 1:2]).then_inc(v_copied, 1)

            step(eng.tensor_tensor(c["d"][:, :], stats[:, :, 1], stats[:, :, 4], op=ALU.subtract))
            step(eng.tensor_tensor(c["m2"][:, :], stats[:, :, 2], stats[:, :, 5], op=ALU.add))
            settle()
            mul(c["d"][:, :], c["d"][:, :], c["d"][:, :])
            settle()
            step(eng.scalar_tensor_tensor(out=c["ve"][:, :], in0=c["d"][:, :], scalar=D / 4.0, in1=c["m2"][:, :],
                                          op0=ALU.mult, op1=ALU.add))
            settle()
            step(eng.tensor_scalar(out=c["ve"][:, :], in0=c["ve"][:, :], scalar1=1.0 / D, scalar2=LN_EPS,
                                   op0=ALU.mult, op1=ALU.add), variance_ready)
            eng.wait_ge(prep_act, PA["rstd0"])
            mul(c["d"][:, :], c["r0"][:, :], c["r0"][:, :])
            settle()
            mul(c["d"][:, :], c["d"][:, :], c["ve"][:, :])
            settle()
            step(eng.tensor_scalar(out=c["d"][:, :], in0=c["d"][:, :], scalar1=-0.5, scalar2=1.5,
                                   op0=ALU.mult, op1=ALU.add))
            settle()
            mul(c["rstd"][:, :], c["d"][:, :], c["r0"][:, :])
            settle()
            mul(c["u1"][:, :], z[:, :, 0], c["rstd"][:, :])
            settle()
            step(eng.tensor_scalar(out=c["u1"][:, :], in0=c["u1"][:, :], scalar1=1.0 + EPS, scalar2=-1.0,
                                   op0=ALU.max, op1=ALU.add))
            settle()
            step(eng.scalar_tensor_tensor(out=pair[:, 0, :], in0=c["u1"][:, :], scalar=2.0, in1=c["u1"][:, :],
                                          op0=ALU.add, op1=ALU.mult))
            for g in range(XG):
                G = slice(g * GB, (g + 1) * GB)
                eng.wait_ge(sqz_done, 2 * g + 2)
                step(eng.tensor_reduce(out=c["zq"][:, G], in_=sqz[:, G, 1:D], axis=AX.X, op=ALU.add))
            settle()
            mul(c["zq"][:, :], c["zq"][:, :], c["rstd"][:, :])
            settle()
            mul(c["zq"][:, :], c["zq"][:, :], c["rstd"][:, :])
            settle()
            step(eng.tensor_scalar(out=pair[:, 1, :], in0=c["zq"][:, :], scalar1=NORM2_MIN, scalar2=ROOT_SCALE,
                                   op0=ALU.max, op1=ALU.mult), roots_ready)
            for g in range(XG - 1):
                G = slice(g * GB, (g + 1) * GB)
                eng.wait_ge(sqH_done, 2 * g + 2)
                step(eng.tensor_reduce(out=c["wq"][:, G], in_=sqH[:, G, 1:D], axis=AX.X, op=ALU.add))
            eng.wait_ge(prep_act, PA["pair"])
            step(eng.reciprocal(pair_r[:, :, :], pair_e[:, :, :]))
            settle()
            mul(pair_r[:, :, :], pair[:, :, :], pair_r[:, :, :])
            settle()
            step(eng.tensor_tensor(pair_r[:, :, :], pair_e[:, :, :], pair_r[:, :, :], op=ALU.add))
            settle()
            step(eng.scalar_tensor_tensor(out=c["w"][:, :], in0=pair_r[:, 0, :], scalar=0.5, in1=c["u1"][:, :],
                                          op0=ALU.mult, op1=ALU.add), acosh1_ready)
            step(eng.reciprocal(c["rn"][:, :], pair_r[:, 1, :]))
            eng.wait_ge(sqH_done, QN)
            G = slice((XG - 1) * GB, NB)
            eng.tensor_reduce(out=c["wq"][:, G], in_=sqH[:, G, 1:D], axis=AX.X, op=ALU.add).then_inc(sqH_done, 1)
            eng.wait_ge(prep_act, PA["acosh1"])
            step(eng.scalar_tensor_tensor(out=c["r"][:, :], in0=c["acosh1"][:, :], scalar=1.0 / HALF_ROOT,
                                          in1=c["rstd"][:, :], op0=ALU.mult, op1=ALU.mult))
            settle()
            mul(c["r"][:, :], c["r"][:, :], c["rn"][:, :])
            settle()
            eng.wait_ge(sqH_done, QN + 1)
            mul(c["n2"][:, :], c["r"][:, :], c["wq"][:, :])
            settle()
            mul(c["n2"][:, :], c["n2"][:, :], c["r"][:, :])
            settle()
            step(eng.tensor_scalar(out=c["n2"][:, :], in0=c["n2"][:, :], scalar1=NORM2_MIN, scalar2=ROOT_SCALE,
                                   op0=ALU.max, op1=ALU.mult), n2_ready)
            eng.wait_ge(prep_act, PA["e_n"])
            step(eng.reciprocal(c["re_n"][:, :], c["e_n"][:, :]))
            settle()
            mul(c["re_n"][:, :], c["n2"][:, :], c["re_n"][:, :])
            settle()
            step(eng.tensor_tensor(c["root_n"][:, :], c["e_n"][:, :], c["re_n"][:, :], op=ALU.add), root_n_ready)
            settle()
            step(eng.reciprocal(c["rn"][:, :], c["root_n"][:, :]))
            eng.wait_ge(prep_act, PA["en"])
            step(eng.reciprocal(c["ren"][:, :], c["en"][:, :]))
            settle()
            step(eng.tensor_tensor(c["sh2"][:, :], c["en"][:, :], c["ren"][:, :], op=ALU.subtract))
            step(eng.tensor_tensor(c["ch"][:, :], c["en"][:, :], c["ren"][:, :], op=ALU.add))
            settle()
            step(eng.tensor_scalar(out=c["ch"][:, :], in0=c["ch"][:, :], scalar1=0.5, scalar2=1.0,
                                   op0=ALU.mult, op1=ALU.add))
            settle()
            step(eng.reciprocal(c["rch"][:, :], c["ch"][:, :]))
            step(eng.scalar_tensor_tensor(out=c["u"][:, :], in0=c["sh2"][:, :], scalar=0.25, in1=c["sh2"][:, :],
                                          op0=ALU.mult, op1=ALU.mult))
            settle()
            mul(c["u"][:, :], c["u"][:, :], c["rch"][:, :])
            step(eng.tensor_scalar(out=c["w"][:, :], in0=c["sh2"][:, :], scalar1=0.5, scalar2=S_EPS,
                                   op0=ALU.mult, op1=ALU.max))
            settle()
            step(eng.scalar_tensor_tensor(out=c["w"][:, :], in0=c["u"][:, :], scalar=EPS, in1=c["w"][:, :],
                                          op0=ALU.max, op1=ALU.add), acosh2_ready)
            eng.wait_ge(prep_act, PA["acosh2"])
            step(eng.scalar_tensor_tensor(out=c["gr"][:, :], in0=c["acosh2"][:, :], scalar=1.0 / HALF_ROOT,
                                          in1=c["rn"][:, :], op0=ALU.mult, op1=ALU.mult))
            settle()
            step(eng.tensor_tensor(c["gr"][:, :], c["gr"][:, :], c["r"][:, :], op=ALU.mult), gr_ready)
            settle()
            mul(c["t"][:, :], c["gr"][:, :], H[:, :, 0])
            settle()
            eng.tensor_reduce(out=tmm[:, 0:1], in_=c["t"][:, :], axis=AX.X, op=ALU.max).then_inc(tmm_done, 1)
            eng.tensor_reduce(out=tmm[:, 1:2], in_=c["t"][:, :], axis=AX.X, op=ALU.min, negate=True).then_inc(tmm_done, 1)

            eng.memset(H[:, :, 0], 1.0).then_inc(ones_done, 1)
            eng.wait_ge(tmmT_done, 1)
            eng.tensor_reduce(out=gmm[:, :], in_=misc[0:1, 0:2 * P].rearrange("o (a p) -> o a p", a=2),
                              axis=AX.X, op=ALU.max).then_inc(gmm_done, 1)
            eng.wait_ge(gmm_all, 1)
            step(eng.tensor_scalar(out=shift[:, :], in0=misc[:, 256:257], scalar1=-1.0, scalar2=SHIFT,
                                   op0=ALU.mult, op1=ALU.add), shift_ready)
            step(eng.tensor_copy(spread[:, :], misc[:, 257:258]))
            settle()
            step(eng.tensor_tensor(spread[:, :], misc[:, 256:257], spread[:, :], op=ALU.add))
            settle()
            eng.tensor_scalar(out=wide[:, :], in0=spread[:, :], scalar1=RANGE_LIMIT, scalar2=None,
                              op0=ALU.is_gt).then_inc(wide_done, 1)
            eng.wait_ge(prep_act, PA["p"])
            step(eng.tensor_scalar(out=w_bf[:, :], in0=c["p"][:, :], scalar1=1e-30, scalar2=None, op0=ALU.max))
            settle()
            step(eng.reciprocal(c["rw"][:, :], w_bf[:, :]))
            settle()
            step(eng.scalar_tensor_tensor(out=c["f"][:, :], in0=c["p"][:, :], scalar=SPLIT_SCALE, in1=c["rw"][:, :],
                                          op0=ALU.mult, op1=ALU.mult), f_ready)
            settle()

            def mask_tile(s, loads, tile, source_blocks):
                eng.wait_ge(raw_in[s], loads)
                if tile is not None:
                    eng.wait_ge(mm_done, tile - MASKS + 1)
                if len(source_blocks) == 2:
                    parts = [(slice(0, 2), j, b) for j, b in enumerate(source_blocks)]
                else:
                    parts = [(i // 2, i % 2, b) for i, b in enumerate(source_blocks)]
                for h, j, b in parts:
                    ins = eng.tensor_scalar(out=mask[:, s % MASKS, h, j, :], in0=rawv[:, s, h, j, :],
                                            scalar1=0.0, scalar2=w_bf[:, b:b + 1], op0=ALU.is_gt, op1=ALU.mult)
                ins.then_inc(masked, 1)

            for k in range(WT):
                eng.wait_ge(hi_done, k + 1)
                for b in (2 * k, 2 * k + 1):
                    eng.scalar_tensor_tensor(out=lo[:, b, :], in0=H[:, b, :], scalar=c["f"][:, b:b + 1],
                                             in1=hi[:, b, :], op0=ALU.mult, op1=ALU.subtract)
                mask_tile(k, 16, k if k >= MASKS else None, (2 * k, 2 * k + 1))

            eng.wait_ge(hsum_done, 1)
            eng.tensor_copy(hmean[:, :], misc[:, 300:301]).then_inc(hmean_done, 1)
            eng.wait_ge(mrow_mm, 1)
            eng.tensor_copy(mean_row[:, :], misc[0:1, 384:384 + P]).then_inc(mrow_done, 1)

            with eng.Fori(1, WIDE_N) as m:
                for k in range(WT):
                    mask_tile(k, m * 16 + 16, m * WT + k, (2 * k, 2 * k + 1))
                    if k in WIDE_STAGES:
                        tail_vector(eng, WIDE_STAGES[k], WIDE_B, m * WIDE_B - WIDE_B, m - 1)
            for i in range(SLIM_N):
                for k in range(ST):
                    mask_tile(i * ST + k, 16 * (WIDE_N + 1), WIDE_N * WT + i * ST + k,
                              tuple(range(4 * k, 4 * k + 4)))
                    if i == 0:
                        tail_vector(eng, SLIM_STAGES[k], WIDE_B, (WIDE_N - 1) * WIDE_B, WIDE_N - 1)
                    else:
                        tail_vector(eng, SLIM_STAGES[k], SLIM_B, WIDE_N * WIDE_B, WIDE_N)
            tail_vector(eng, range(9), SLIM_B, NB - SLIM_B, CHUNKS - 1)

            eng.wait_ge(wide_done, 1)
            go = eng.value_load(wide[0:1, 0:1], min_val=0, max_val=1)
            with eng.If(go == 1):
                eng.nop().then_inc(g_free, 1)

                def unit(u):
                    with eng.Fori(0, WT) as k:
                        eng.wait_ge(g_raw, u * (16 * WT) + k * 16 + 16)
                        eng.tensor_copy(tG[:, :], c["t"][:, bass.ds(k * 2, 2)]).then_inc(g_step, 1)
                        eng.tensor_scalar(out=fillG, in0=rawG, scalar1=0.0, scalar2=MASK_FILL,
                                          op0=ALU.is_le, op1=ALU.mult).then_inc(g_step, 1)
                        eng.wait_ge(g_step, u * (3 * WT) + k * 3 + 2)
                        for j in range(2):
                            ins = eng.tensor_scalar(out=eG[:, j, :], in0=rawG[:, j * HALF:(j + 1) * HALF], scalar1=0.0,
                                                    scalar2=tG[:, j:j + 1], op0=ALU.is_gt, op1=ALU.mult)
                        ins.then_inc(g_step, 1)
                        eng.wait_ge(g_step, u * (3 * WT) + k * 3 + 3)
                        eng.nop().then_inc(g_free, 1)
                        eng.tensor_tensor(eG, eG, fillG.rearrange("p (j i) -> p j i", j=2), op=ALU.add).then_inc(g_e, 1)
                        eng.wait_ge(g_tp, u * WT + k + 1)
                        for b in range(SLIM_B):
                            ins = eng.tensor_copy(sG[:, b, bass.ds(k * (2 * P), 2 * P)], tpG[b][:, 0:2 * P])
                        ins.then_inc(g_max, 1)
                    eng.wait_ge(g_max, u * (WT + 1) + WT)
                    eng.tensor_reduce(out=nmG[:, :], in_=sG, axis=AX.X, op=ALU.max, negate=True).then_inc(g_max, 1)
                    eng.wait_ge(g_exp, u + 1)
                    eng.memset(accG, 0.0).then_inc(g_acc, 1)
                    with eng.Fori(0, NB) as b:
                        eng.tensor_copy(pG, sG[:, :, bass.ds(b * P, P)]).then_inc(g_col, 1)
                        eng.tensor_copy(hG, H[:, bass.ds(b, 1), :].rearrange("p a d -> p (a d)")).then_inc(g_col, 1)
                        eng.wait_ge(g_colT, u * NB + b + 1)
                        eng.tensor_copy(pTG, spare[:, :]).then_inc(g_pT, 1)
                        eng.wait_ge(g_mm, u * NB + b + 1)
                        eng.wait_ge(g_acc, u * (NB + 1) + b + 1)
                        eng.tensor_tensor(accG, acc_slim[0][:, :], accG, op=ALU.add).then_inc(g_acc, 1)
                    tail_vector(eng, range(9), SLIM_B, u * SLIM_B, u, CHUNKS)

                with eng.Fori(0, WIDE_N) as m:
                    for h in range(2):
                        unit(m * 2 + h)
                with eng.Fori(0, SLIM_N) as m:
                    unit(m + 2 * WIDE_N)

        @block.scalar
        def _(eng):
            c = col
            done = []
            eng.wait_ge(zero_done, 3)
            eng.dma_start(waT[:, :], w_att_t).then_inc(const_in, 16)
            eng.dma_start(a2s[:, :], a2).then_inc(const_in, 16)
            eng.dma_start(wgT[1:P, 1:P], w_gcn_t).then_inc(const_in, 16)
            eng.dma_start(wg[1:P, 1:P], w_gcn).then_inc(const_in, 16)
            eng.dma_start(wa[1:P, 1:P], w_att[1:P, 1:P]).then_inc(att_in, 16)

            def step(ins, name):
                done.append(name)
                assert PA[name] == len(done)
                ins.then_inc(prep_act, 1)

            def own(name):
                eng.wait_ge(prep_act, PA[name])

            def copy_H(u):
                B = slice(u * QB, (u + 1) * QB)
                eng.wait_ge(zw_done, u + 1)
                eng.activation(H[:, B, :], zw_ring[u % 3].rearrange("p (b d) -> p b d", d=D),
                               ACT.Copy).then_inc(H_done, 1)

            def square_H(u):
                B = slice(u * QB, (u + 1) * QB)
                eng.wait_ge(H_done, u + 1)
                eng.activation(sqH[:, B, :], H[:, B, :], ACT.Square).then_inc(sqH_done, 1)

            U = QN
            eng.preload_act_table_set("natural_log_exp_and_others")
            for u in range(U):
                B = slice(u * QB, (u + 1) * QB)
                eng.wait_ge(tp_done, u + 1)
                eng.activation(zT[:, B, :], tp_ring[u % 4].rearrange("p (b d) -> p b d", d=D),
                               ACT.Copy).then_inc(zT_done, 1)
                eng.wait_ge(z_done, u + 1)
                eng.activation(sqz[:, B, :], z[:, B, :], ACT.Square).then_inc(sqz_done, 1)
                if u >= 1:
                    copy_H(u - 1)
                if u >= 2:
                    square_H(u - 2)
                if u == U - 2:
                    eng.wait_ge(variance_ready, 1)
                    step(eng.activation(c["lv"][:, :], c["ve"][:, :], ACT.Ln), "ln_ve")
                    own("ln_ve")
                    step(eng.activation(c["r0"][:, :], c["lv"][:, :], ACT.Exp, scale=-0.5), "rstd0")
            copy_H(U - 1)
            square_H(U - 2)
            square_H(U - 1)
            eng.wait_ge(roots_ready, 1)
            step(eng.activation(pair_e[:, :, :], pair[:, :, :], ACT.Ln), "ln_pair")
            own("ln_pair")
            step(eng.activation(pair_e[:, :, :], pair_e[:, :, :], ACT.Exp, scale=0.5), "pair")
            eng.wait_ge(acosh1_ready, 1)
            step(eng.activation(c["acosh1"][:, :], c["w"][:, :], ACT.Ln, bias=1.0), "acosh1")
            eng.wait_ge(n2_ready, 1)
            step(eng.activation(c["ln_n"][:, :], c["n2"][:, :], ACT.Ln), "ln_n")
            own("ln_n")
            step(eng.activation(c["e_n"][:, :], c["ln_n"][:, :], ACT.Exp, scale=0.5), "e_n")
            eng.wait_ge(root_n_ready, 1)
            step(eng.activation(c["en"][:, :], c["root_n"][:, :], ACT.Exp, scale=HALF_ROOT), "en")
            eng.wait_ge(acosh2_ready, 1)
            step(eng.activation(c["acosh2"][:, :], c["w"][:, :], ACT.Ln, bias=1.0), "acosh2")

            def scale_rows(first, last):
                for b in range(first, last):
                    ins = eng.activation(H[:, b, 1:D], H[:, b, 1:D], ACT.Copy, scale=c["gr"][:, b:b + 1])
                ins.then_inc(H_scaled, last - first)

            eng.wait_ge(gr_ready, 1)
            scale_rows(0, 4)
            scale_rows(4, 8)
            eng.wait_ge(shift_ready, 1)
            step(eng.activation(c["p"][:, :], c["t"][:, :], ACT.Exp, bias=shift[:, :]), "p")
            eng.wait_ge(f_ready, 1)
            eng.wait_ge(ones_done, 1)
            for k in range(WT):
                if 2 * k + 8 < NB:
                    scale_rows(2 * k + 8, 2 * k + 10)
                eng.wait_ge(H_scaled, 2 * k + 2)
                for b in (2 * k, 2 * k + 1):
                    ins = eng.activation(hi[:, b, :], H[:, b, :], ACT.Copy, scale=c["f"][:, b:b + 1])
                ins.then_inc(hi_done, 1)

            wide_acc = acc_wide[:, :, :].rearrange("p h i -> p (h i)")
            tail_scalar(eng, WIDE_B, wide_acc, mm_done, WT, 0)
            with eng.Fori(1, WIDE_N) as m:
                tail_scalar(eng, WIDE_B, wide_acc, mm_done, m * WT + WT, m)
            for i in range(SLIM_N):
                tail_scalar(eng, SLIM_B, acc_slim[i][:, :], mm_done, WIDE_N * WT + (i + 1) * ST, WIDE_N + i)

            eng.wait_ge(wide_done, 1)
            go = eng.value_load(wide[0:1, 0:1], min_val=0, max_val=1)
            with eng.If(go == 1):
                def unit(u):
                    eng.wait_ge(g_max, u * (WT + 1) + (WT + 1))
                    for b in range(SLIM_B):
                        ins = eng.activation(sG[:, b, :], sG[:, b, :], ACT.Exp, bias=nmG[:, b:b + 1])
                    ins.then_inc(g_exp, 1)
                    tail_scalar(eng, SLIM_B, accG, g_acc, u * (NB + 1) + (NB + 1), u, CHUNKS)

                with eng.Fori(0, WIDE_N) as m:
                    for h in range(2):
                        unit(m * 2 + h)
                with eng.Fori(0, SLIM_N) as m:
                    unit(m + 2 * WIDE_N)

        @block.tensor
        def _(eng):
            eng.wait_ge(const_in, 64)
            nc.tensor.matmul(misc[:, 0:1], waT[:, :], a2s[:, :], start=True, stop=True).then_inc(v_mm, 1)
            eng.wait_ge(ident_done, 2)

            def transpose_z(u):
                eng.wait_ge(z_done, u + 1)
                if u >= 4:
                    eng.wait_ge(zT_done, u - 3)
                for b in range(QB):
                    ins = nc.tensor.transpose(tp_ring[u % 4][:, b * P:(b + 1) * P], z[:, u * QB + b, :], ident[:, :])
                ins.then_inc(tp_done, 1)

            def product(u):
                eng.wait_ge(zT_done, u + 1)
                if u >= 3:
                    eng.wait_ge(H_done, u - 2)
                for b in range(QB):
                    ins = nc.tensor.matmul(zw_ring[u % 3][:, b * P:(b + 1) * P], zT[:, u * QB + b, :], wg[:, :],
                                           start=True, stop=True)
                ins.then_inc(zw_done, 1)

            U = QN
            transpose_z(0)
            transpose_z(1)
            eng.wait_ge(v_copied, 1)
            nc.tensor.matmul(misc[:, 1:2], wgT[:, :], v_sb[:, :], start=True, stop=True).then_inc(v_mm, 1)
            eng.wait_ge(v_copied, 2)
            for u in range(2, U + 2):
                if u < U:
                    transpose_z(u)
                product(u - 2)

            eng.wait_ge(tmm_done, 2)
            nc.tensor.transpose(misc[0:1, 0:P], tmm[:, 0:1], ident[:, :])
            nc.tensor.transpose(misc[0:1, P:2 * P], tmm[:, 1:2], ident[:, :]).then_inc(tmmT_done, 1)
            eng.wait_ge(gmm_done, 1)
            eng.wait_ge(const_done, 3)
            nc.tensor.matmul(misc[:, 256:258], ones_row[:, :], gmm[:, :], start=True, stop=True).then_inc(gmm_all, 1)
            eng.wait_ge(wide_done, 1)

            def tile(s, tile_no, source_blocks, banks):
                eng.wait_ge(masked, tile_no + 1)
                for i, b in enumerate(source_blocks):
                    for part in (hi, lo):
                        for h in range(len(banks)):
                            m = mask[:, s % MASKS, h, i, :] if len(banks) == 2 else mask[:, s % MASKS, i // 2, i % 2, :]
                            ins = nc.tensor.matmul(banks[h], part[:, b, :], m, start=(part is hi and b == 0),
                                                   stop=(part is lo and b == NB - 1))
                ins.then_inc(mm_done, 1)

            wide_banks = [acc_wide[:, 0, :], acc_wide[:, 1, :]]
            eng.wait_ge(const_done, 3)
            for k in range(WT):
                tile(k, k, (2 * k, 2 * k + 1), wide_banks)
                for b in (2 * k, 2 * k + 1):
                    ins = nc.tensor.matmul(misc[:, 300:301], H[:, b, :], inv_n[:, :],
                                           start=(b == 0), stop=(b == NB - 1))
            ins.then_inc(hsum_done, 1)
            eng.wait_ge(hmean_done, 1)
            eng.wait_ge(att_in, 16)
            nc.tensor.matmul(misc[0:1, 384:384 + P], hmean[:, :], wa[:, :], start=True, stop=True).then_inc(mrow_mm, 1)
            eng.wait_ge(mrow_done, 1)

            with eng.Fori(1, WIDE_N) as m:
                eng.wait_ge(tail_act, m * NA - (NA - A["acc"]))
                for k in range(WT):
                    tile(k, m * WT + k, (2 * k, 2 * k + 1), wide_banks)
                    if k == 0:
                        tail_tensor(eng, WIDE_B, m - 1)
            for i in range(SLIM_N):
                for k in range(ST):
                    tile(i * ST + k, WIDE_N * WT + i * ST + k, tuple(range(4 * k, 4 * k + 4)), [acc_slim[i][:, :]])
                    if k == 0:
                        tail_tensor(eng, SLIM_B if i else WIDE_B, WIDE_N - 1 + i)
            tail_tensor(eng, SLIM_B, CHUNKS - 1)

            go = eng.value_load(wide[0:1, 0:1], min_val=0, max_val=1)
            with eng.If(go == 1):
                def unit(u):
                    with eng.Fori(0, WT) as k:
                        eng.wait_ge(g_e, u * WT + k + 1)
                        for b in range(SLIM_B):
                            for j in range(2):
                                ins = nc.tensor.transpose(tpG[b][:, j * P:(j + 1) * P],
                                                          eG[:, j, b * P:(b + 1) * P], ident[:, :])
                        ins.then_inc(g_tp, 1)
                    with eng.Fori(0, NB) as b:
                        eng.wait_ge(g_col, u * (2 * NB) + b * 2 + 2)
                        for q in range(SLIM_B):
                            ins = nc.tensor.transpose(spare[:, q * P:(q + 1) * P], pG[:, q, :], ident[:, :])
                        ins.then_inc(g_colT, 1)
                        eng.wait_ge(g_pT, u * NB + b + 1)
                        nc.tensor.matmul(acc_slim[0][:, :], hG, pTG, start=True, stop=True).then_inc(g_mm, 1)
                    tail_tensor(eng, SLIM_B, u, CHUNKS)

                with eng.Fori(0, WIDE_N) as m:
                    for h in range(2):
                        unit(m * 2 + h)
                with eng.Fori(0, SLIM_N) as m:
                    unit(m + 2 * WIDE_N)


PA = {n: i + 1 for i, n in enumerate(
    ["ln_ve", "rstd0", "ln_pair", "pair", "acosh1", "ln_n", "e_n", "en", "acosh2", "p"])}

_INS = ["x", "adj_t", "w_gcn", "w_gcn_t", "w_att", "w_att_t", "a2"]


def kernel(**inputs):
    import numpy as _np
    import concourse.bacc as _bacc
    from concourse import mybir as _mybir
    from concourse.bass_utils import run_bass_kernel_spmd as _run

    adj = _np.asarray(inputs["adj"])
    w_gcn = _np.asarray(inputs["L0_gnn_W_gcn"])
    w_att = _np.asarray(inputs["L0_gnn_W_att"])
    a = adj.reshape(P, NB, P, NB)
    wide_rows = a[:, :WIDE_N * WIDE_B].reshape(P, WIDE_N, 2, 4, P, WT, 2)
    slim_rows = a[:, WIDE_N * WIDE_B:].reshape(P, SLIM_N, SLIM_B, P, ST, 2, 2)
    wide_tiles = wide_rows.transpose(1, 5, 4, 2, 6, 3, 0).reshape(WIDE_N * WT, P, TILE)
    slim_tiles = slim_rows.transpose(1, 4, 3, 5, 6, 2, 0).reshape(SLIM_N * ST, P, TILE)
    host = {
        "x": inputs["x"],
        "adj_t": _np.concatenate([wide_tiles, slim_tiles]),
        "w_gcn": w_gcn, "w_gcn_t": w_gcn.T, "w_att": w_att, "w_att_t": w_att.T,
        "a2": _np.asarray(inputs["L0_gnn_a_att"])[D:],
    }
    nc = _bacc.Bacc("TRN2", target_bir_lowering=False, num_devices=1)
    arrays, args = {}, []
    for name in _INS:
        a = _np.ascontiguousarray(host[name])
        arrays[f"in_{name}_dram"] = a
        args.append(nc.dram_tensor(f"in_{name}_dram", a.shape, _mybir.dt.from_np(a.dtype), kind="ExternalInput").ap())
    args.append(nc.dram_tensor("out_0_dram", (N, D), _mybir.dt.float32, kind="ExternalOutput").ap())
    build(nc, *args)
    r = _run(nc, [arrays], core_ids=[0])
    return r.results[0]["out_0_dram"]
```

```python
import math
from contextlib import ExitStack

import concourse.bass as bass
from concourse import mybir

N, D = 4096, 128
P = 128
NB = N // P
HALF = 512
TILE = 2048
HT = TILE // 2
WIDE_B, SLIM_B = 8, 4
WIDE_N, SLIM_N = 3, 2
CHUNKS = WIDE_N + SLIM_N
WT = NB // 2
ST = NB // 4
TILES = WIDE_N * WT + SLIM_N * ST
SLOTS = WT
MASKS = 4
UNITS = 2 * WIDE_N + SLIM_N
QB = HALF // P
QN = NB // QB
ACT_SQUARES = 4
XG = 4
GB = NB // XG
LN_EPS = 1e-5
EPS = 2.0 ** -23
S_EPS = math.sqrt(EPS * (EPS + 2.0))
NORM2_MIN = 1e-30
ROOT_SCALE = 2.0 ** 40
HALF_ROOT = 2.0 ** -21
MASK_FILL = -9000000000000000.0
SHIFT = 60.0
RANGE_LIMIT = 125.0
SPLIT_SCALE = 512.0

V = {n: i + 1 for i, n in enumerate(
    ["rden0", "rden1", "em0", "y0", "em1", "y1", "q1", "lift", "one_q", "re", "quot", "root", "u", "m", "w",
     "ryn", "f", "fy", "ssq", "ns", "re2", "quot2", "root2", "rn", "ren", "hsum", "diff", "F", "col0",
     "o0", "o1"])}
A = {n: i + 1 for i, n in enumerate(
    ["acc0", "acc1", "e0", "e1", "q0", "ln1", "exp1", "ln_w", "sig0", "sig1", "ssq0", "ln2", "exp2", "exp_n"])}
NV, NA = len(V), len(A)
STAGES = 9
SLIM_T1 = [0, 0]
WIDE_STAGES = {5: [0], 6: [1], 8: [2], 9: [3], 10: [4], 13: [5], 14: [6], 15: [7, 8]}
SLIM_STAGES = [
    {2: [0], 3: [1], 4: [2, 3, 4], 6: [5], 7: [6, 7, 8]},
    {1: [0], 2: [1], 3: [2], 4: [3], 5: [4], 6: [5], 7: [6, 7]}]


def build(nc, x, adj_t, w_gcn, w_att, a2, out):
    f32, bf16, f16, i32 = mybir.dt.float32, mybir.dt.bfloat16, mybir.dt.float16, mybir.dt.int32
    ALU, ACT, AX = mybir.AluOpType, mybir.ActivationFunctionType, mybir.AxisListType

    x_blocks = x.rearrange("(p b) d -> p b d", b=NB)
    out_blocks = out.rearrange("(p b) d -> p b d", b=NB)
    halves = adj_t.rearrange("t p (h n) -> t h p n", h=2)

    with ExitStack() as ctx:
        def sb(name, shape, dt):
            return ctx.enter_context(nc.sbuf_tensor(name, shape, dt))

        def sem(name):
            return ctx.enter_context(nc.semaphore(name))

        raw = sb("raw", [P, SLOTS, TILE], i32)
        xs = sb("xs", [P, NB, D], f32)
        H = sb("H", [P, NB, D], f32)
        split = sb("split", [P, 2, NB, D], f16)
        hi, lo = split[:, 0], split[:, 1]
        masks = sb("masks", [P, MASKS, TILE], bf16)
        mask = masks[:, :, :].rearrange("p s (h j i) -> p s h j i", h=2, j=2)
        rawv = raw[:, :, :].rearrange("p s (h j i) -> p s h j i", h=2, j=2)

        arena = masks[:, 2:MASKS, :].rearrange("p s n -> p (s n)").bitcast(f32)
        used = [0]

        def prep(width):
            used[0] += width
            return arena[:, used[0] - width:used[0]]

        def raw_f32(first, slots):
            return raw[:, first:first + slots, :].rearrange("p s n -> p (s n)").bitcast(f32)

        z = raw_f32(SLOTS - 6, 2).rearrange("p (b d) -> p b d", d=D)
        sqz = raw_f32(SLOTS - 4, 2).rearrange("p (b d) -> p b d", d=D)
        sqH = raw_f32(SLOTS - 2, 2).rearrange("p (b d) -> p b d", d=D)
        zT = split[:, :, :, :].rearrange("p a b d -> p (a b d)").bitcast(f32).rearrange("p (b d) -> p b d", d=D)

        accS = sb("accS", [P, WIDE_B * P], f32)
        E = sb("E", [P, WIDE_B, D], f32)
        y = sb("y", [P, WIDE_B, D], f32)
        sq, sig = E, y
        mean_rest = y[0:1, 0:3, :]
        empty = E[0:1, :, :].rearrange("o b d -> o (b d)").bitcast(bf16)

        ident = sb("ident", [P, P], f32)
        wg = prep(P)
        wgT = prep(P)
        wa = sb("wa", [P, P], f32)
        waT = prep(P)
        a2s = prep(1)
        v_sb = prep(1)
        ones_row = prep(P)[0:1, :]
        inv_n = sb("inv_n", [P, 1], f32)
        hmean = sb("hmean", [P, 1], f32)
        mean_parts = sb("mean_parts", [1, 3, P], bf16)
        stats = prep(NB * 6).rearrange("p (b n) -> p b n", n=6)
        col = {n: prep(NB) for n in
               ["msum", "mean", "d", "m2", "ve", "lv", "r0", "rstd", "u1", "zq", "acosh1", "r",
                "wq", "n2", "ln_n", "e_n", "re_n", "root_n", "en", "ren", "sh2", "ch2",
                "u", "w", "acosh2", "rn", "rw"]}
        col |= {n: sb("c_" + n, [P, NB], f32) for n in ["gr", "t", "p", "f"]}
        pair = prep(2 * NB).rearrange("p (a b) -> p a b", a=2)
        pair_e = prep(2 * NB).rearrange("p (a b) -> p a b", a=2)
        pair_r = prep(2 * NB).rearrange("p (a b) -> p a b", a=2)
        w_bf = sb("w_bf", [P, NB], bf16)
        tmm = prep(2)
        gmm = sb("gmm", [1, 2], f32)
        shift = prep(1)
        spread = prep(1)
        wide = sb("wide", [P, 1], i32)
        small = {n: sb("s_" + n, [P, WIDE_B], f32) for n in
                 ["rden", "q", "u", "m", "w", "acosh", "ryn", "f", "ssq", "ns",
                  "ln2", "e2", "re2", "quot2", "root2", "rn", "en", "ren", "diff", "F", "hsum"]}
        sp = sb("sp", [P, 2, WIDE_B], f32)
        sp_e = sb("sp_e", [P, 2, WIDE_B], f32)
        sp_r = sb("sp_r", [P, 2, WIDE_B], f32)
        sp_s = sb("sp_s", [P, 2, WIDE_B], f32)
        rawG = raw[:, 0, 0:HT]
        eG = raw_f32(1, 1)[:, 0:HT].rearrange("p (j i) -> p j i", j=2)
        fillG = raw_f32(2, 1)[:, 0:HT]
        mixG = raw_f32(3, 1)
        pG = mixG[:, 0:HALF].rearrange("p (b j) -> p b j", b=SLIM_B)
        pTG = mixG[:, HALF:2 * HALF]
        accG = mixG[:, 2 * HALF:3 * HALF]
        hG = mixG[:, 3 * HALF:3 * HALF + D]
        sG = raw_f32(8, 8).rearrange("p (b j) -> p b j", b=SLIM_B)
        tG = sb("tG", [P, 2], f32)
        nmG = sb("nmG", [P, SLIM_B], f32)

        def psum(name, shape):
            return ctx.enter_context(nc.psum_tensor(name, shape, f32))

        acc_wide = psum("acc_wide", [P, 2, HALF])
        Z = psum("Z", [P, 2, QB, D])
        acc_slim = [psum(f"acc_slim{i}", [P, HALF]) for i in range(2)]
        spare = psum("spare", [P, HALF])
        misc = psum("misc", [P, HALF])
        tp_ring = [acc_wide[:, 0, :], acc_wide[:, 1, :], Z[:, 0].rearrange("p b d -> p (b d)"),
                   Z[:, 1].rearrange("p b d -> p (b d)")]
        zw_ring = [acc_slim[0][:, :], acc_slim[1][:, :], spare[:, :]]
        tpG = [acc_wide[:, 0, :], acc_wide[:, 1, :], acc_slim[0][:, :], acc_slim[1][:, :]]

        x_in = [sem(f"x_in{g}") for g in range(XG)]
        raw_in = [sem(f"raw_in{s}") for s in range(SLOTS)]
        last_in = [sem(f"last_in{h}") for h in range(2)]
        last_masked = sem("last_masked")
        stored = sem("stored")
        x_again = sem("x_again")
        att_in = sem("att_in")
        gcn_in = sem("gcn_in")
        wT_mm = sem("wT_mm")
        wT_copied = sem("wT_copied")
        const_done = sem("const_done")
        zero_done = sem("zero_done")
        ident_done = sem("ident_done")
        prep_dve = sem("prep_dve")
        prep_act = sem("prep_act")
        variance_ready = sem("variance_ready")
        roots_ready = sem("roots_ready")
        acosh1_ready = sem("acosh1_ready")
        n2_ready = sem("n2_ready")
        root_n_ready = sem("root_n_ready")
        acosh2_ready = sem("acosh2_ready")
        gr_ready = sem("gr_ready")
        shift_ready = sem("shift_ready")
        f_ready = sem("f_ready")
        hi_done = sem("hi_done")
        v_mm = sem("v_mm")
        v_copied = sem("v_copied")
        tp_done = sem("tp_done")
        zT_done = sem("zT_done")
        zw_done = sem("zw_done")
        H_done = sem("H_done")
        sqz_done = sem("sqz_done")
        sqH_done = sem("sqH_done")
        z_done = sem("z_done")
        H_scaled = sem("H_scaled")
        tmm_done = sem("tmm_done")
        tmmT_done = sem("tmmT_done")
        gmm_done = sem("gmm_done")
        gmm_all = sem("gmm_all")
        ones_done = sem("ones_done")
        wide_done = sem("wide_done")
        masked = sem("masked")
        mm_done = sem("mm_done")
        hsum_done = sem("hsum_done")
        hmean_done = sem("hmean_done")
        mrow_mm = sem("mrow_mm")
        mrow_copied = sem("mrow_copied")
        mrow_done = sem("mrow_done")
        tail_dve = sem("tail_dve")
        tail_act = sem("tail_act")
        tail_mm = sem("tail_mm")
        tail_flag = sem("tail_flag")
        g_raw = sem("g_raw")
        g_free = sem("g_free")
        g_step = sem("g_step")
        g_e = sem("g_e")
        g_tp = sem("g_tp")
        g_max = sem("g_max")
        g_exp = sem("g_exp")
        g_col = sem("g_col")
        g_colT = sem("g_colT")
        g_pT = sem("g_pT")
        g_mm = sem("g_mm")
        g_acc = sem("g_acc")

        block = ctx.enter_context(nc.Block())

        @block.sync
        def _(eng):
            def load_x(g):
                G = slice(g * GB, (g + 1) * GB)
                eng.dma_start(xs[:, G, :], x_blocks[:, G, :]).then_inc(x_in[g], 16)

            load_x(0)
            load_x(1)
            eng.dma_start(wa[:, :], w_att).then_inc(att_in, 16)
            eng.dma_start(a2s[:, :], a2).then_inc(att_in, 16)
            load_x(2)
            eng.wait_ge(zero_done, 1)
            eng.dma_start(wg[1:P, 1:P], w_gcn).then_inc(gcn_in, 16)
            load_x(3)

            def load(tile, s):
                eng.dma_start(raw[:, s, :], adj_t[tile]).then_inc(raw_in[s], 16)

            def store(chunk, first, blocks, step="o1"):
                eng.wait_ge(tail_dve, NV * chunk + V[step])
                B = slice(first, first + blocks)
                eng.dma_start(out_blocks[:, B, :], xs[:, B, :]).then_inc(stored, 16)

            for s in range(SLOTS - 6):
                load(s, s)
            eng.wait_ge(tp_done, QN)
            eng.wait_ge(roots_ready, 1)
            for s in range(SLOTS - 6, SLOTS - 2):
                load(s, s)
            eng.wait_ge(sqH_done, QN)
            for s in range(SLOTS - 2, SLOTS):
                load(s, s)
            with eng.Fori(1, WIDE_N) as c:
                for k in range(WT):
                    eng.wait_ge(masked, c * WT - WT + k + 1)
                    load(c * WT + k, k)
            for s in range(SLOTS):
                tile = WIDE_N * WT + s
                eng.wait_ge(masked, tile - SLOTS + 1)
                if tile < TILES - 1:
                    load(tile, s)
                else:
                    for h in range(2):
                        eng.dma_start(raw[:, s, h * HT:(h + 1) * HT], halves[tile, h]).then_inc(last_in[h], 16)
            for c in range(WIDE_N):
                store(c, c * WIDE_B, WIDE_B)
            for c in range(SLIM_N - 1):
                store(WIDE_N + c, WIDE_N * WIDE_B + c * SLIM_B, SLIM_B)
            for h in range(2):
                store(CHUNKS - 1, NB - SLIM_B + h * SLIM_B // 2, SLIM_B // 2, step=f"o{h}")
            eng.wait_ge(stored, 16 * (CHUNKS + 1))

            eng.wait_ge(wide_done, 1)
            go = eng.value_load(wide[0:1, 0:1], min_val=0, max_val=1)
            with eng.If(go == 1):
                eng.dma_start(xs[:, :, :], x_blocks).then_inc(x_again, 16)

                def unit(u, first, sides):
                    n = len(sides)
                    with eng.Fori(0, WT // n) as k:
                        for i, side in enumerate(sides):
                            eng.wait_ge(g_free, u * WT + k * n + (i + 1))
                            eng.dma_start(rawG, halves[first + k, side]).then_inc(g_raw, 16)
                    eng.wait_ge(tail_dve, u * NV + NV * (CHUNKS + 1))
                    eng.dma_start(out_blocks[:, bass.ds(u * SLIM_B, SLIM_B), :],
                                  xs[:, bass.ds(u * SLIM_B, SLIM_B), :]).then_inc(stored, 16)

                with eng.Fori(0, WIDE_N) as c:
                    for h in range(2):
                        unit(c * 2 + h, c * WT, [h])
                with eng.Fori(0, SLIM_N) as c:
                    unit(c + 2 * WIDE_N, c * ST + WIDE_N * WT, [0, 1])
                eng.wait_ge(stored, 16 * (CHUNKS + 1 + UNITS))


        def Z_block(n, b):
            return Z[:, b // (n // 2), b % (n // 2), :]

        def flags(n, h):
            return empty[:, h * n * P:h * n * P + n * P // 2]

        def tail_vector(eng, stages, n, block0, c, extra=0):
            s = {k: v[:, 0:n] for k, v in small.items()}
            vb, ab = c * NV + extra * NV, c * NA + extra * NA
            halves_of = [range(h * n // 2, (h + 1) * n // 2) for h in range(2)]
            lean = not (isinstance(c, int) and c + extra == CHUNKS - 1)

            def own(name):
                eng.wait_ge(tail_dve, vb + V[name])

            def step(ins, steps=1):
                ins.then_inc(tail_dve, steps)

            def square_sums(source, sums, blocks):
                for b in blocks:
                    ins = eng.scalar_tensor_tensor(out=sq[:, b, 1:D], in0=source[:, b, 1:D], scalar=1.0,
                                                   in1=source[:, b, 1:D], op0=ALU.mult, op1=ALU.mult,
                                                   accum_out=s[sums][:, b:b + 1])
                if blocks[-1] == n - 1:
                    step(ins)

            rows = xs[:, bass.ds(block0, n), :]

            def result_rows(h):
                for b in halves_of[h]:
                    ins = eng.scalar_tensor_tensor(out=rows[:, b, 1:D], in0=sig[:, b, 1:D],
                                                   scalar=s["F"][:, b:b + 1], in1=rows[:, b, 1:D],
                                                   op0=ALU.mult, op1=ALU.add)
                step(ins)

            if 0 in stages:
                for h in range(2):
                    eng.wait_ge(tail_mm, c * 2 + (extra * 2 + h + 1))
                    step(eng.reciprocal(s["rden"][:, h * n // 2:(h + 1) * n // 2], Z[:, h, 0:n // 2, 0]))
            if 1 in stages:
                for h, blocks in enumerate(halves_of):
                    eng.wait_ge(tail_act, ab + A[f"e{h}"])
                    B = slice(blocks[0], blocks[-1] + 1)
                    step(eng.tensor_scalar(out=E[:, B, :], in0=E[:, B, :], scalar1=1.0, scalar2=-1.0,
                                           op0=ALU.min, op1=ALU.add))
                    own(f"em{h}")
                    for b in blocks:
                        ins = eng.scalar_tensor_tensor(out=y[:, b, :], in0=Z_block(n, b), scalar=s["rden"][:, b:b + 1],
                                                       in1=E[:, b, :], op0=ALU.mult, op1=ALU.max)
                    step(ins, 2 if h == 1 and lean else 1)
                if not lean:
                    own("y1")
                    square_sums(y, "q", halves_of[1])
            if 2 in stages:
                eng.wait_ge(tail_act, ab + A["q0"])
                own("q1")
                step(eng.tensor_scalar(out=sp[:, 0, 0:n], in0=s["q"], scalar1=NORM2_MIN, scalar2=ROOT_SCALE,
                                       op0=ALU.max, op1=ALU.mult))
                step(eng.tensor_scalar(out=sp[:, 1, 0:n], in0=s["q"], scalar1=1.0, scalar2=None, op0=ALU.add))
            if 3 in stages:
                eng.wait_ge(tail_act, ab + A["exp1"])
                step(eng.reciprocal(sp_r[:, :, 0:n], sp_e[:, :, 0:n]))
                own("re")
                step(eng.tensor_tensor(sp_r[:, :, 0:n], sp[:, :, 0:n], sp_r[:, :, 0:n], op=ALU.mult))
                own("quot")
                step(eng.tensor_tensor(sp_s[:, :, 0:n], sp_e[:, :, 0:n], sp_r[:, :, 0:n], op=ALU.add))
                own("root")
                step(eng.tensor_scalar(out=s["u"], in0=sp_s[:, 1, 0:n], scalar1=0.5, scalar2=-1.0,
                                       op0=ALU.mult, op1=ALU.add))
                step(eng.tensor_scalar(out=s["m"], in0=sp_s[:, 0, 0:n], scalar1=HALF_ROOT, scalar2=S_EPS,
                                       op0=ALU.mult, op1=ALU.max))
                own("m")
                step(eng.scalar_tensor_tensor(out=s["w"], in0=s["u"], scalar=EPS, in1=s["m"],
                                              op0=ALU.max, op1=ALU.add))
                step(eng.reciprocal(s["ryn"], sp_s[:, 0, 0:n]))
            if 4 in stages:
                eng.wait_ge(tail_act, ab + A["ln_w"])
                own("ryn")
                step(eng.scalar_tensor_tensor(out=s["f"], in0=s["acosh"], scalar=1.0 / HALF_ROOT,
                                              in1=s["ryn"], op0=ALU.mult, op1=ALU.mult),
                     2 if lean else 1)
                if not lean:
                    own("f")
                    for b in range(n):
                        ins = eng.tensor_scalar(out=y[:, b, :], in0=y[:, b, :], scalar1=s["f"][:, b:b + 1],
                                                scalar2=None, op0=ALU.mult)
                    step(ins)
            if 5 in stages:
                for h, blocks in enumerate(halves_of):
                    eng.wait_ge(tail_act, ab + A[f"sig{h}"])
                    if h == 1 or not lean:
                        square_sums(sig, "ssq", blocks)
                eng.wait_ge(tail_act, ab + A["ssq0"])
                own("ssq")
                step(eng.tensor_scalar(out=s["ns"], in0=s["ssq"], scalar1=NORM2_MIN, scalar2=ROOT_SCALE,
                                       op0=ALU.max, op1=ALU.mult))
            if 6 in stages:
                eng.wait_ge(tail_act, ab + A["exp2"])
                step(eng.reciprocal(s["re2"], s["e2"]))
                own("re2")
                step(eng.tensor_tensor(s["quot2"], s["ns"], s["re2"], op=ALU.mult))
                own("quot2")
                step(eng.tensor_tensor(s["root2"], s["e2"], s["quot2"], op=ALU.add))
                own("root2")
                step(eng.reciprocal(s["rn"], s["root2"]))
            if 7 in stages:
                eng.wait_ge(tail_act, ab + A["exp_n"])
                step(eng.reciprocal(s["ren"], s["en"]))
                own("ren")
                step(eng.tensor_tensor(s["hsum"], s["en"], s["ren"], op=ALU.add))
                step(eng.tensor_tensor(s["diff"], s["en"], s["ren"], op=ALU.subtract))
                own("diff")
                step(eng.scalar_tensor_tensor(out=s["F"], in0=s["diff"], scalar=0.5 / HALF_ROOT, in1=s["rn"],
                                              op0=ALU.mult, op1=ALU.mult))
                if extra:
                    eng.wait_ge(x_again, 16)
                step(eng.scalar_tensor_tensor(out=rows[:, :, 0], in0=s["hsum"], scalar=0.5, in1=rows[:, :, 0],
                                              op0=ALU.mult, op1=ALU.add))
                own("F")
                result_rows(0)
            if 8 in stages:
                result_rows(1)

        def tail_scalar(eng, n, acc_src, acc_sem, acc_val, c, extra=0):
            s = {k: v[:, 0:n] for k, v in small.items()}
            vb, ab = c * NV + extra * NV, c * NA + extra * NA
            halves_of = [range(h * n // 2, (h + 1) * n // 2) for h in range(2)]
            lean = not (isinstance(c, int) and c + extra == CHUNKS - 1)

            def step(ins, steps=1):
                ins.then_inc(tail_act, steps)

            if extra or not isinstance(c, int) or c > 0:
                eng.wait_ge(tail_mm, c * 2 + extra * 2)
            eng.wait_ge(acc_sem, acc_val)
            for h in range(2):
                I = slice(h * n * P // 2, (h + 1) * n * P // 2)
                step(eng.activation(accS[:, I], acc_src[:, I], ACT.Copy))
            for h, blocks in enumerate(halves_of):
                eng.wait_ge(tail_dve, vb + V[f"rden{h}"])
                for b in blocks:
                    ins = eng.activation(E[:, b, :], Z_block(n, b), ACT.Exp, scale=s["rden"][:, b:b + 1])
                step(ins)
            def square_sums(source, sums, blocks):
                for b in blocks:
                    ins = eng.activation(sq[:, b, 1:D], source[:, b, 1:D], ACT.Square, accum_out=s[sums][:, b:b + 1])
                return ins

            eng.wait_ge(tail_dve, vb + V["y0"])
            ins = square_sums(y, "q", halves_of[0])
            if lean:
                eng.wait_ge(tail_dve, vb + V["y1"])
                ins = square_sums(y, "q", halves_of[1])
            step(ins)
            eng.wait_ge(tail_dve, vb + V["one_q"])
            step(eng.activation(sp_e[:, :, 0:n], sp[:, :, 0:n], ACT.Ln))
            eng.wait_ge(tail_act, ab + A["ln1"])
            step(eng.activation(sp_e[:, :, 0:n], sp_e[:, :, 0:n], ACT.Exp, scale=0.5))
            eng.wait_ge(tail_dve, vb + V["w"])
            step(eng.activation(s["acosh"], s["w"], ACT.Ln, bias=1.0))
            eng.wait_ge(tail_dve, vb + V["fy"])
            for h, blocks in enumerate(halves_of):
                if lean:
                    for b in blocks:
                        ins = eng.activation(sig[:, b, :], y[:, b, :], ACT.Sigmoid, scale=s["f"][:, b:b + 1])
                    step(ins)
                else:
                    B = slice(blocks[0], blocks[-1] + 1)
                    step(eng.activation(sig[:, B, :], y[:, B, :], ACT.Sigmoid), 1 + h)
            if lean:
                eng.wait_ge(tail_act, ab + A["sig0"])
                step(square_sums(sig, "ssq", halves_of[0]))
            eng.preload_act_table_set("natural_log_exp_and_others")
            eng.wait_ge(tail_dve, vb + V["ns"])
            step(eng.activation(s["ln2"], s["ns"], ACT.Ln))
            eng.wait_ge(tail_act, ab + A["ln2"])
            step(eng.activation(s["e2"], s["ln2"], ACT.Exp, scale=0.5))
            eng.wait_ge(tail_dve, vb + V["root2"])
            step(eng.activation(s["en"], s["root2"], ACT.Exp, scale=HALF_ROOT))

        def tail_flags(eng, n, c, extra=0):
            for h in range(2):
                I = slice(h * n * P // 2, (h + 1) * n * P // 2)
                eng.wait_ge(tail_act, c * NA + (extra * NA + A[f"acc{h}"]))
                eng.tensor_scalar(out=flags(n, h), in0=accS[0:1, I], scalar1=0.0,
                                  scalar2=None, op0=ALU.is_equal).then_inc(tail_flag, 1)

        def tail_tensor(eng, n, c, extra=0):
            for h in range(2):
                blocks = range(h * n // 2, (h + 1) * n // 2)
                eng.wait_ge(tail_act, c * NA + (extra * NA + A[f"acc{h}"]))
                for b in blocks:
                    nc.tensor.matmul(Z_block(n, b), accS[:, b * P:(b + 1) * P], wa[:, :],
                                     start=(b == blocks[0]), stop=False)
                eng.wait_ge(tail_flag, c * 2 + (extra * 2 + h + 1))
                for q, b in enumerate(blocks):
                    for i in range(3):
                        last = nc.tensor.matmul(Z_block(n, b), flags(n, h)[:, q * P:(q + 1) * P], mean_parts[:, i, :],
                                                start=False, stop=(b == blocks[-1] and i == 2))
                last.then_inc(tail_mm, 1)

        @block.gpsimd
        def _(eng):
            eng.memset(ident[:, :], 0.0).then_inc(ident_done, 1)
            eng.memset(wg[:, :], 0.0).then_inc(zero_done, 1)
            eng.wait_ge(ident_done, 1)
            eng.affine_select(out=ident[:, :], in_=ident[:, :], compare_op=ALU.not_equal, fill=1.0,
                              base=0, pattern=[[-1, P]], channel_multiplier=1).then_inc(ident_done, 1)
            eng.memset(ones_row[:, :], 1.0).then_inc(const_done, 1)
            eng.memset(inv_n[:, :], 1.0 / N).then_inc(const_done, 1)
            for u in range(QN):
                B = slice(u * QB, (u + 1) * QB)
                eng.wait_ge(z_done, u + 1)
                eng.tensor_tensor(sqz[:, B, :], z[:, B, :], z[:, B, :], op=ALU.mult).then_inc(sqz_done, 1)

            eng.wait_ge(wT_mm, 1)
            eng.memset(wa[:, 0:1], 0.0).then_inc(zero_done, 1)
            eng.memset(wa[0:1, 1:P], 0.0).then_inc(zero_done, 1)
            eng.wait_ge(zero_done, 3)
            eng.memset(wa[0:1, 0:1], 1.0).then_inc(const_done, 1)

            eng.wait_ge(mrow_copied, 1)
            for i in range(3):
                if i > 0:
                    eng.tensor_tensor(mean_rest[:, i, :], mean_rest[:, i - 1, :], mean_parts[:, i - 1, :],
                                      op=ALU.subtract).then_inc(mrow_done, 1)
                    eng.wait_ge(mrow_done, 2 * i)
                eng.tensor_copy(mean_parts[:, i, :], mean_rest[:, i, :]).then_inc(mrow_done, 1)
                if i < 2:
                    eng.wait_ge(mrow_done, 2 * i + 1)

            for c in range(CHUNKS - 1):
                tail_flags(eng, WIDE_B if c < WIDE_N else SLIM_B, c)

            eng.wait_ge(wide_done, 1)
            go = eng.value_load(wide[0:1, 0:1], min_val=0, max_val=1)
            with eng.If(go == 1):
                for u in range(UNITS):
                    tail_flags(eng, SLIM_B, u, CHUNKS)

        @block.vector
        def _(eng):
            c = col
            n = [0]
            last = [prep_dve, 0]

            def step(ins, signal=None):
                n[0] += signal is None
                last[:] = [signal, 1] if signal is not None else [prep_dve, n[0]]
                ins.then_inc(last[0], 1)

            def settle():
                eng.wait_ge(last[0], last[1])

            def mul(dst, a, b):
                step(eng.tensor_tensor(dst, a, b, op=ALU.mult))

            for g in range(XG):
                G = slice(g * GB, (g + 1) * GB)
                eng.wait_ge(x_in[g], 16)
                for b in range(g * GB, (g + 1) * GB):
                    step(eng.bn_stats(stats[:, b, :], xs[:, b, :]))
                settle()
                step(eng.tensor_tensor(c["msum"][:, G], stats[:, G, 1], stats[:, G, 4], op=ALU.add))
                settle()
                step(eng.tensor_scalar(out=c["mean"][:, G], in0=c["msum"][:, G], scalar1=0.5, scalar2=None, op0=ALU.mult))
                settle()
                for b in range(g * GB, (g + 1) * GB):
                    ins = eng.tensor_scalar(out=z[:, b, :], in0=xs[:, b, :], scalar1=c["mean"][:, b:b + 1], scalar2=0.0,
                                            op0=ALU.subtract, op1=ALU.max)
                    if b % QB == QB - 1:
                        ins.then_inc(z_done, 1)

            step(eng.tensor_tensor(c["d"][:, :], stats[:, :, 1], stats[:, :, 4], op=ALU.subtract))
            step(eng.tensor_tensor(c["m2"][:, :], stats[:, :, 2], stats[:, :, 5], op=ALU.add))
            settle()
            mul(c["d"][:, :], c["d"][:, :], c["d"][:, :])
            settle()
            step(eng.scalar_tensor_tensor(out=c["ve"][:, :], in0=c["d"][:, :], scalar=D / 4.0, in1=c["m2"][:, :],
                                          op0=ALU.mult, op1=ALU.add))
            settle()
            step(eng.tensor_scalar(out=c["ve"][:, :], in0=c["ve"][:, :], scalar1=1.0 / D, scalar2=LN_EPS,
                                   op0=ALU.mult, op1=ALU.add), variance_ready)
            for g in range(XG):
                G = slice(g * GB, (g + 1) * GB)
                eng.wait_ge(sqz_done, 2 * g + 2)
                step(eng.tensor_reduce(out=c["zq"][:, G], in_=sqz[:, G, 1:D], axis=AX.X, op=ALU.add))
            eng.wait_ge(prep_act, PA["rstd0"])
            mul(c["d"][:, :], c["r0"][:, :], c["r0"][:, :])
            settle()
            mul(c["d"][:, :], c["d"][:, :], c["ve"][:, :])
            settle()
            step(eng.tensor_scalar(out=c["d"][:, :], in0=c["d"][:, :], scalar1=-0.5, scalar2=1.5,
                                   op0=ALU.mult, op1=ALU.add))
            settle()
            mul(c["rstd"][:, :], c["d"][:, :], c["r0"][:, :])
            settle()
            mul(c["u1"][:, :], z[:, :, 0], c["rstd"][:, :])
            settle()
            step(eng.tensor_scalar(out=c["u1"][:, :], in0=c["u1"][:, :], scalar1=1.0 + EPS, scalar2=-1.0,
                                   op0=ALU.max, op1=ALU.add))
            settle()
            step(eng.scalar_tensor_tensor(out=pair[:, 0, :], in0=c["u1"][:, :], scalar=2.0, in1=c["u1"][:, :],
                                          op0=ALU.add, op1=ALU.mult))
            settle()
            mul(c["zq"][:, :], c["zq"][:, :], c["rstd"][:, :])
            settle()
            mul(c["zq"][:, :], c["zq"][:, :], c["rstd"][:, :])
            settle()
            step(eng.tensor_scalar(out=pair[:, 1, :], in0=c["zq"][:, :], scalar1=NORM2_MIN, scalar2=ROOT_SCALE,
                                   op0=ALU.max, op1=ALU.mult), roots_ready)
            def square_H(u):
                eng.wait_ge(H_done, u + 1)
                for b in range(u * QB, (u + 1) * QB):
                    ins = eng.scalar_tensor_tensor(out=sqH[:, b, 1:D], in0=H[:, b, 1:D], scalar=1.0, in1=H[:, b, 1:D],
                                                   op0=ALU.mult, op1=ALU.mult, accum_out=c["wq"][:, b:b + 1])
                ins.then_inc(sqH_done, 1)

            for u in range(ACT_SQUARES, QN - 2):
                square_H(u)
            eng.wait_ge(prep_act, PA["pair"])
            step(eng.reciprocal(pair_r[:, :, :], pair_e[:, :, :]))
            settle()
            mul(pair_r[:, :, :], pair[:, :, :], pair_r[:, :, :])
            settle()
            step(eng.tensor_tensor(pair_r[:, :, :], pair_e[:, :, :], pair_r[:, :, :], op=ALU.add))
            settle()
            step(eng.scalar_tensor_tensor(out=c["w"][:, :], in0=pair_r[:, 0, :], scalar=0.5, in1=c["u1"][:, :],
                                          op0=ALU.mult, op1=ALU.add), acosh1_ready)
            step(eng.reciprocal(c["rn"][:, :], pair_r[:, 1, :]))
            for u in range(QN - 2, QN):
                square_H(u)
            eng.wait_ge(prep_act, PA["acosh1"])
            step(eng.scalar_tensor_tensor(out=c["r"][:, :], in0=c["acosh1"][:, :], scalar=1.0 / HALF_ROOT,
                                          in1=c["rstd"][:, :], op0=ALU.mult, op1=ALU.mult))
            settle()
            mul(c["r"][:, :], c["r"][:, :], c["rn"][:, :])
            settle()
            eng.wait_ge(sqH_done, QN)
            mul(c["n2"][:, :], c["r"][:, :], c["wq"][:, :])
            settle()
            mul(c["n2"][:, :], c["n2"][:, :], c["r"][:, :])
            settle()
            step(eng.tensor_scalar(out=c["n2"][:, :], in0=c["n2"][:, :], scalar1=NORM2_MIN, scalar2=ROOT_SCALE,
                                   op0=ALU.max, op1=ALU.mult), n2_ready)
            eng.wait_ge(prep_act, PA["e_n"])
            step(eng.reciprocal(c["re_n"][:, :], c["e_n"][:, :]))
            settle()
            mul(c["re_n"][:, :], c["n2"][:, :], c["re_n"][:, :])
            settle()
            step(eng.tensor_tensor(c["root_n"][:, :], c["e_n"][:, :], c["re_n"][:, :], op=ALU.add), root_n_ready)
            settle()
            step(eng.reciprocal(c["rn"][:, :], c["root_n"][:, :]))
            eng.wait_ge(prep_act, PA["en"])
            step(eng.reciprocal(c["ren"][:, :], c["en"][:, :]))
            settle()
            step(eng.tensor_tensor(c["ch2"][:, :], c["en"][:, :], c["ren"][:, :], op=ALU.add))
            step(eng.tensor_tensor(c["sh2"][:, :], c["en"][:, :], c["ren"][:, :], op=ALU.subtract))
            settle()
            step(eng.tensor_scalar(out=c["u"][:, :], in0=c["ch2"][:, :], scalar1=0.5, scalar2=-1.0,
                                   op0=ALU.mult, op1=ALU.add))
            step(eng.tensor_scalar(out=c["w"][:, :], in0=c["sh2"][:, :], scalar1=0.5, scalar2=S_EPS,
                                   op0=ALU.mult, op1=ALU.max))
            settle()
            step(eng.scalar_tensor_tensor(out=c["w"][:, :], in0=c["u"][:, :], scalar=EPS, in1=c["w"][:, :],
                                          op0=ALU.max, op1=ALU.add), acosh2_ready)
            eng.wait_ge(prep_act, PA["acosh2"])
            step(eng.scalar_tensor_tensor(out=c["gr"][:, :], in0=c["acosh2"][:, :], scalar=1.0 / HALF_ROOT,
                                          in1=c["rn"][:, :], op0=ALU.mult, op1=ALU.mult))
            settle()
            step(eng.tensor_tensor(c["gr"][:, :], c["gr"][:, :], c["r"][:, :], op=ALU.mult), gr_ready)
            settle()
            mul(c["t"][:, :], c["gr"][:, :], H[:, :, 0])
            settle()
            eng.tensor_reduce(out=tmm[:, 0:1], in_=c["t"][:, :], axis=AX.X, op=ALU.max).then_inc(tmm_done, 1)
            eng.tensor_reduce(out=tmm[:, 1:2], in_=c["t"][:, :], axis=AX.X, op=ALU.min, negate=True).then_inc(tmm_done, 1)

            eng.memset(H[:, :, 0], 1.0).then_inc(ones_done, 1)
            eng.wait_ge(tmmT_done, 1)
            eng.tensor_reduce(out=gmm[:, :], in_=misc[0:1, 0:2 * P].rearrange("o (a p) -> o a p", a=2),
                              axis=AX.X, op=ALU.max).then_inc(gmm_done, 1)
            eng.wait_ge(gmm_all, 1)
            step(eng.tensor_scalar(out=shift[:, :], in0=misc[:, 256:257], scalar1=-1.0, scalar2=SHIFT,
                                   op0=ALU.mult, op1=ALU.add), shift_ready)
            step(eng.tensor_copy(spread[:, :], misc[:, 257:258]))
            settle()
            step(eng.tensor_tensor(spread[:, :], misc[:, 256:257], spread[:, :], op=ALU.add))
            settle()
            eng.tensor_scalar(out=wide[:, :], in0=spread[:, :], scalar1=RANGE_LIMIT, scalar2=None,
                              op0=ALU.is_gt).then_inc(wide_done, 1)
            eng.wait_ge(prep_act, PA["p"])
            step(eng.tensor_scalar(out=w_bf[:, :], in0=c["p"][:, :], scalar1=1e-30, scalar2=None, op0=ALU.max))
            settle()
            step(eng.reciprocal(c["rw"][:, :], w_bf[:, :]))
            settle()
            step(eng.scalar_tensor_tensor(out=c["f"][:, :], in0=c["p"][:, :], scalar=SPLIT_SCALE, in1=c["rw"][:, :],
                                          op0=ALU.mult, op1=ALU.mult), f_ready)
            settle()

            def mask_tile(s, loads, tile, source_blocks):
                if loads is not None:
                    eng.wait_ge(raw_in[s], loads)
                if tile is not None:
                    eng.wait_ge(mm_done, tile - MASKS + 1)
                if len(source_blocks) == 2:
                    parts = [(slice(0, 2), j, b) for j, b in enumerate(source_blocks)]
                else:
                    parts = [(i // 2, i % 2, b) for i, b in enumerate(source_blocks)]
                for h, j, b in parts:
                    if loads is None:
                        eng.wait_ge(last_in[h], 16)
                    ins = eng.tensor_scalar(out=mask[:, s % MASKS, h, j, :], in0=rawv[:, s, h, j, :],
                                            scalar1=0.0, scalar2=w_bf[:, b:b + 1], op0=ALU.is_gt, op1=ALU.mult)
                    if loads is None:
                        ins.then_inc(last_masked, 1)
                if loads is not None:
                    ins.then_inc(masked, 1)

            for k in range(WT):
                eng.wait_ge(hi_done, k + 1)
                for b in (2 * k, 2 * k + 1):
                    eng.scalar_tensor_tensor(out=lo[:, b, :], in0=H[:, b, :], scalar=c["f"][:, b:b + 1],
                                             in1=hi[:, b, :], op0=ALU.mult, op1=ALU.subtract)
                mask_tile(k, 16, k if k >= MASKS else None, (2 * k, 2 * k + 1))

            with eng.Fori(1, WIDE_N) as m:
                for k in range(WT):
                    mask_tile(k, m * 16 + 16, m * WT + k, (2 * k, 2 * k + 1))
                    if k in WIDE_STAGES:
                        tail_vector(eng, WIDE_STAGES[k], WIDE_B, m * WIDE_B - WIDE_B, m - 1)
            for i in range(SLIM_N):
                for k in range(ST):
                    t = WIDE_N * WT + i * ST + k
                    mask_tile(i * ST + k, 16 * (WIDE_N + 1) if t < TILES - 1 else None, t,
                              tuple(range(4 * k, 4 * k + 4)))
                    if k in SLIM_STAGES[i] and i == 0:
                        tail_vector(eng, SLIM_STAGES[i][k], WIDE_B, (WIDE_N - 1) * WIDE_B, WIDE_N - 1)
                    elif k in SLIM_STAGES[i]:
                        tail_vector(eng, SLIM_STAGES[i][k], SLIM_B, WIDE_N * WIDE_B, WIDE_N)
            tail_flags(eng, SLIM_B, CHUNKS - 1)
            tail_vector(eng, [8], SLIM_B, WIDE_N * WIDE_B, WIDE_N)
            tail_vector(eng, range(STAGES), SLIM_B, NB - SLIM_B, CHUNKS - 1)

            eng.wait_ge(wide_done, 1)
            go = eng.value_load(wide[0:1, 0:1], min_val=0, max_val=1)
            with eng.If(go == 1):
                eng.nop().then_inc(g_free, 1)

                def unit(u):
                    with eng.Fori(0, WT) as k:
                        eng.wait_ge(g_raw, u * (16 * WT) + k * 16 + 16)
                        eng.tensor_copy(tG[:, :], c["t"][:, bass.ds(k * 2, 2)]).then_inc(g_step, 1)
                        eng.tensor_scalar(out=fillG, in0=rawG, scalar1=0.0, scalar2=MASK_FILL,
                                          op0=ALU.is_le, op1=ALU.mult).then_inc(g_step, 1)
                        eng.wait_ge(g_step, u * (3 * WT) + k * 3 + 2)
                        for j in range(2):
                            ins = eng.tensor_scalar(out=eG[:, j, :], in0=rawG[:, j * HALF:(j + 1) * HALF], scalar1=0.0,
                                                    scalar2=tG[:, j:j + 1], op0=ALU.is_gt, op1=ALU.mult)
                        ins.then_inc(g_step, 1)
                        eng.wait_ge(g_step, u * (3 * WT) + k * 3 + 3)
                        eng.nop().then_inc(g_free, 1)
                        eng.tensor_tensor(eG, eG, fillG.rearrange("p (j i) -> p j i", j=2), op=ALU.add).then_inc(g_e, 1)
                        eng.wait_ge(g_tp, u * WT + k + 1)
                        for b in range(SLIM_B):
                            ins = eng.tensor_copy(sG[:, b, bass.ds(k * (2 * P), 2 * P)], tpG[b][:, 0:2 * P])
                        ins.then_inc(g_max, 1)
                    eng.wait_ge(g_max, u * (WT + 1) + WT)
                    eng.tensor_reduce(out=nmG[:, :], in_=sG, axis=AX.X, op=ALU.max, negate=True).then_inc(g_max, 1)
                    eng.wait_ge(g_exp, u + 1)
                    eng.memset(accG, 0.0).then_inc(g_acc, 1)
                    with eng.Fori(0, NB) as b:
                        eng.tensor_copy(pG, sG[:, :, bass.ds(b * P, P)]).then_inc(g_col, 1)
                        eng.tensor_copy(hG, H[:, bass.ds(b, 1), :].rearrange("p a d -> p (a d)")).then_inc(g_col, 1)
                        eng.wait_ge(g_colT, u * NB + b + 1)
                        eng.tensor_copy(pTG, spare[:, :]).then_inc(g_pT, 1)
                        eng.wait_ge(g_mm, u * NB + b + 1)
                        eng.wait_ge(g_acc, u * (NB + 1) + b + 1)
                        eng.tensor_tensor(accG, acc_slim[0][:, :], accG, op=ALU.add).then_inc(g_acc, 1)
                    tail_vector(eng, range(STAGES), SLIM_B, u * SLIM_B, u, CHUNKS)

                with eng.Fori(0, WIDE_N) as m:
                    for h in range(2):
                        unit(m * 2 + h)
                with eng.Fori(0, SLIM_N) as m:
                    unit(m + 2 * WIDE_N)

        @block.scalar
        def _(eng):
            c = col
            done = []
            def step(ins, name):
                done.append(name)
                assert PA[name] == len(done)
                ins.then_inc(prep_act, 1)

            def own(name):
                eng.wait_ge(prep_act, PA[name])

            def copy_H(u):
                B = slice(u * QB, (u + 1) * QB)
                eng.wait_ge(zw_done, u + 1)
                eng.activation(H[:, B, :], zw_ring[u % 3].rearrange("p (b d) -> p b d", d=D),
                               ACT.Copy).then_inc(H_done, 1)

            def square_H(u):
                eng.wait_ge(H_done, u + 1)
                for b in range(u * QB, (u + 1) * QB):
                    ins = eng.activation(sqH[:, b, 1:D], H[:, b, 1:D], ACT.Square, accum_out=c["wq"][:, b:b + 1])
                ins.then_inc(sqH_done, 1)

            U = QN
            eng.preload_act_table_set("natural_log_exp_and_others")
            def copy_zT(u):
                B = slice(u * QB, (u + 1) * QB)
                eng.wait_ge(tp_done, u + 1)
                eng.activation(zT[:, B, :], tp_ring[u % 4].rearrange("p (b d) -> p b d", d=D),
                               ACT.Copy).then_inc(zT_done, 1)

            def copy_w(dst, src, made, count, copied):
                eng.wait_ge(made, count)
                eng.activation(dst, src, ACT.Copy).then_inc(copied, 1)

            copy_w(waT[:, :], misc[:, P:2 * P], wT_mm, 1, wT_copied)
            copy_w(v_sb[:, :], misc[:, 0:1], v_mm, 1, v_copied)
            copy_w(wgT[:, :], misc[:, P:2 * P], wT_mm, 2, wT_copied)
            copy_zT(0)
            copy_w(wg[:, 0:1], misc[:, 1:2], v_mm, 2, v_copied)
            copy_zT(1)
            copy_zT(2)
            for u in range(U):
                if u + 3 < U:
                    copy_zT(u + 3)
                copy_H(u)
                if u == U - 3:
                    eng.wait_ge(variance_ready, 1)
                    step(eng.activation(c["lv"][:, :], c["ve"][:, :], ACT.Ln), "ln_ve")
                    own("ln_ve")
                    step(eng.activation(c["r0"][:, :], c["lv"][:, :], ACT.Exp, scale=-0.5), "rstd0")
            for u in range(ACT_SQUARES - 1):
                square_H(u)
            eng.wait_ge(roots_ready, 1)
            step(eng.activation(pair_e[:, :, :], pair[:, :, :], ACT.Ln), "ln_pair")
            own("ln_pair")
            step(eng.activation(pair_e[:, :, :], pair_e[:, :, :], ACT.Exp, scale=0.5), "pair")
            square_H(ACT_SQUARES - 1)
            eng.wait_ge(acosh1_ready, 1)
            step(eng.activation(c["acosh1"][:, :], c["w"][:, :], ACT.Ln, bias=1.0), "acosh1")
            eng.wait_ge(n2_ready, 1)
            step(eng.activation(c["ln_n"][:, :], c["n2"][:, :], ACT.Ln), "ln_n")
            own("ln_n")
            step(eng.activation(c["e_n"][:, :], c["ln_n"][:, :], ACT.Exp, scale=0.5), "e_n")
            eng.wait_ge(root_n_ready, 1)
            step(eng.activation(c["en"][:, :], c["root_n"][:, :], ACT.Exp, scale=HALF_ROOT), "en")
            eng.wait_ge(acosh2_ready, 1)
            step(eng.activation(c["acosh2"][:, :], c["w"][:, :], ACT.Ln, bias=1.0), "acosh2")

            def scale_rows(first, last):
                for b in range(first, last):
                    ins = eng.activation(H[:, b, 1:D], H[:, b, 1:D], ACT.Copy, scale=c["gr"][:, b:b + 1])
                ins.then_inc(H_scaled, last - first)

            eng.wait_ge(gr_ready, 1)
            scale_rows(0, 4)
            scale_rows(4, 8)
            eng.wait_ge(shift_ready, 1)
            step(eng.activation(c["p"][:, :], c["t"][:, :], ACT.Exp, bias=shift[:, :]), "p")
            eng.wait_ge(f_ready, 1)
            eng.wait_ge(ones_done, 1)
            for k in range(WT):
                eng.wait_ge(H_scaled, 2 * k + 2)
                for b in (2 * k, 2 * k + 1):
                    ins = eng.activation(hi[:, b, :], H[:, b, :], ACT.Copy, scale=c["f"][:, b:b + 1])
                ins.then_inc(hi_done, 1)
                if 2 * k + 8 < NB:
                    scale_rows(2 * k + 8, 2 * k + 10)

            eng.wait_ge(hsum_done, 1)
            eng.activation(hmean[:, :], misc[:, 300:301], ACT.Copy).then_inc(hmean_done, 1)
            eng.wait_ge(mrow_mm, 1)
            eng.activation(mean_rest[:, 0, :], misc[0:1, 384:384 + P], ACT.Copy).then_inc(mrow_copied, 1)

            wide_acc = acc_wide[:, :, :].rearrange("p h i -> p (h i)")
            tail_scalar(eng, WIDE_B, wide_acc, mm_done, WT, 0)
            with eng.Fori(1, WIDE_N) as m:
                tail_scalar(eng, WIDE_B, wide_acc, mm_done, m * WT + WT, m)
            for i in range(SLIM_N):
                tail_scalar(eng, SLIM_B, acc_slim[i][:, :], mm_done, WIDE_N * WT + (i + 1) * ST, WIDE_N + i)

            eng.wait_ge(wide_done, 1)
            go = eng.value_load(wide[0:1, 0:1], min_val=0, max_val=1)
            with eng.If(go == 1):
                def unit(u):
                    eng.wait_ge(g_max, u * (WT + 1) + (WT + 1))
                    for b in range(SLIM_B):
                        ins = eng.activation(sG[:, b, :], sG[:, b, :], ACT.Exp, bias=nmG[:, b:b + 1])
                    ins.then_inc(g_exp, 1)
                    tail_scalar(eng, SLIM_B, accG, g_acc, u * (NB + 1) + (NB + 1), u, CHUNKS)

                with eng.Fori(0, WIDE_N) as m:
                    for h in range(2):
                        unit(m * 2 + h)
                with eng.Fori(0, SLIM_N) as m:
                    unit(m + 2 * WIDE_N)

        @block.tensor
        def _(eng):
            eng.wait_ge(ident_done, 2)
            eng.wait_ge(att_in, 32)
            nc.tensor.transpose(misc[:, P:2 * P], wa[:, :], ident[:, :]).then_inc(wT_mm, 1)

            def transpose_z(u):
                eng.wait_ge(z_done, u + 1)
                if u >= 4:
                    eng.wait_ge(zT_done, u - 3)
                for b in range(QB):
                    ins = nc.tensor.transpose(tp_ring[u % 4][:, b * P:(b + 1) * P], z[:, u * QB + b, :], ident[:, :])
                ins.then_inc(tp_done, 1)

            def product(u):
                eng.wait_ge(zT_done, u + 1)
                if u >= 3:
                    eng.wait_ge(H_done, u - 2)
                for b in range(QB):
                    ins = nc.tensor.matmul(zw_ring[u % 3][:, b * P:(b + 1) * P], zT[:, u * QB + b, :], wg[:, :],
                                           start=True, stop=True)
                ins.then_inc(zw_done, 1)

            U = QN
            eng.wait_ge(wT_copied, 1)
            nc.tensor.matmul(misc[:, 0:1], waT[:, :], a2s[:, :], start=True, stop=True).then_inc(v_mm, 1)
            eng.wait_ge(gcn_in, 16)
            eng.wait_ge(v_copied, 1)
            nc.tensor.transpose(misc[:, P:2 * P], wg[:, :], ident[:, :]).then_inc(wT_mm, 1)
            transpose_z(0)
            eng.wait_ge(wT_copied, 2)
            nc.tensor.matmul(misc[:, 1:2], wgT[:, :], v_sb[:, :], start=True, stop=True).then_inc(v_mm, 1)
            transpose_z(1)
            transpose_z(2)
            transpose_z(3)
            eng.wait_ge(v_copied, 2)
            for u in range(U):
                product(u)
                if u + 4 < U:
                    transpose_z(u + 4)

            eng.wait_ge(tmm_done, 2)
            nc.tensor.transpose(misc[0:1, 0:P], tmm[:, 0:1], ident[:, :])
            nc.tensor.transpose(misc[0:1, P:2 * P], tmm[:, 1:2], ident[:, :]).then_inc(tmmT_done, 1)
            eng.wait_ge(gmm_done, 1)
            eng.wait_ge(const_done, 3)
            nc.tensor.matmul(misc[:, 256:258], ones_row[:, :], gmm[:, :], start=True, stop=True).then_inc(gmm_all, 1)
            eng.wait_ge(wide_done, 1)

            def tile(s, tile_no, source_blocks, banks):
                last = isinstance(tile_no, int) and tile_no == TILES - 1
                if not last:
                    eng.wait_ge(masked, tile_no + 1)
                for i, b in enumerate(source_blocks):
                    if last:
                        eng.wait_ge(last_masked, i + 1)
                    for part in (hi, lo):
                        for h in range(len(banks)):
                            m = mask[:, s % MASKS, h, i, :] if len(banks) == 2 else mask[:, s % MASKS, i // 2, i % 2, :]
                            ins = nc.tensor.matmul(banks[h], part[:, b, :], m, start=(part is hi and b == 0),
                                                   stop=(part is lo and b == NB - 1))
                ins.then_inc(mm_done, 1)

            wide_banks = [acc_wide[:, 0, :], acc_wide[:, 1, :]]
            eng.wait_ge(const_done, 3)
            for k in range(WT):
                tile(k, k, (2 * k, 2 * k + 1), wide_banks)
                for b in (2 * k, 2 * k + 1):
                    ins = nc.tensor.matmul(misc[:, 300:301], H[:, b, :], inv_n[:, :],
                                           start=(b == 0), stop=(b == NB - 1))
            ins.then_inc(hsum_done, 1)
            eng.wait_ge(hmean_done, 1)
            nc.tensor.matmul(misc[0:1, 384:384 + P], hmean[:, :], wa[:, :], start=True, stop=True).then_inc(mrow_mm, 1)

            with eng.Fori(1, WIDE_N) as m:
                eng.wait_ge(tail_act, m * NA - (NA - A["acc1"]))
                for k in range(WT):
                    tile(k, m * WT + k, (2 * k, 2 * k + 1), wide_banks)
                    if k == 0:
                        eng.wait_ge(mrow_done, 5)
                        tail_tensor(eng, WIDE_B, m - 1)
            for i in range(SLIM_N):
                for k in range(ST):
                    if k == SLIM_T1[i]:
                        tail_tensor(eng, SLIM_B if i else WIDE_B, WIDE_N - 1 + i)
                    tile(i * ST + k, WIDE_N * WT + i * ST + k, tuple(range(4 * k, 4 * k + 4)), [acc_slim[i][:, :]])
            tail_tensor(eng, SLIM_B, CHUNKS - 1)

            go = eng.value_load(wide[0:1, 0:1], min_val=0, max_val=1)
            with eng.If(go == 1):
                def unit(u):
                    with eng.Fori(0, WT) as k:
                        eng.wait_ge(g_e, u * WT + k + 1)
                        for b in range(SLIM_B):
                            for j in range(2):
                                ins = nc.tensor.transpose(tpG[b][:, j * P:(j + 1) * P],
                                                          eG[:, j, b * P:(b + 1) * P], ident[:, :])
                        ins.then_inc(g_tp, 1)
                    with eng.Fori(0, NB) as b:
                        eng.wait_ge(g_col, u * (2 * NB) + b * 2 + 2)
                        for q in range(SLIM_B):
                            ins = nc.tensor.transpose(spare[:, q * P:(q + 1) * P], pG[:, q, :], ident[:, :])
                        ins.then_inc(g_colT, 1)
                        eng.wait_ge(g_pT, u * NB + b + 1)
                        nc.tensor.matmul(acc_slim[0][:, :], hG, pTG, start=True, stop=True).then_inc(g_mm, 1)
                    tail_tensor(eng, SLIM_B, u, CHUNKS)

                with eng.Fori(0, WIDE_N) as m:
                    for h in range(2):
                        unit(m * 2 + h)
                with eng.Fori(0, SLIM_N) as m:
                    unit(m + 2 * WIDE_N)


PA = {n: i + 1 for i, n in enumerate(
    ["ln_ve", "rstd0", "ln_pair", "pair", "acosh1", "ln_n", "e_n", "en", "acosh2", "p"])}

_INS = ["x", "adj_t", "w_gcn", "w_att", "a2"]


def kernel(**inputs):
    import numpy as _np
    import concourse.bacc as _bacc
    from concourse import mybir as _mybir
    from concourse.bass_utils import run_bass_kernel_spmd as _run

    adj = _np.asarray(inputs["adj"])
    w_gcn = _np.asarray(inputs["L0_gnn_W_gcn"])
    w_att = _np.asarray(inputs["L0_gnn_W_att"])
    a = adj.reshape(P, NB, P, NB)
    wide_rows = a[:, :WIDE_N * WIDE_B].reshape(P, WIDE_N, 2, 4, P, WT, 2)
    slim_rows = a[:, WIDE_N * WIDE_B:].reshape(P, SLIM_N, SLIM_B, P, ST, 2, 2)
    wide_tiles = wide_rows.transpose(1, 5, 4, 2, 6, 3, 0).reshape(WIDE_N * WT, P, TILE)
    slim_tiles = slim_rows.transpose(1, 4, 3, 5, 6, 2, 0).reshape(SLIM_N * ST, P, TILE)
    host = {
        "x": inputs["x"],
        "adj_t": _np.concatenate([wide_tiles, slim_tiles]),
        "w_gcn": w_gcn, "w_att": w_att,
        "a2": _np.asarray(inputs["L0_gnn_a_att"])[D:],
    }
    nc = _bacc.Bacc("TRN2", target_bir_lowering=False, num_devices=1)
    arrays, args = {}, []
    for name in _INS:
        a = _np.ascontiguousarray(host[name])
        arrays[f"in_{name}_dram"] = a
        args.append(nc.dram_tensor(f"in_{name}_dram", a.shape, _mybir.dt.from_np(a.dtype), kind="ExternalInput").ap())
    args.append(nc.dram_tensor("out_0_dram", (N, D), _mybir.dt.float32, kind="ExternalOutput").ap())
    build(nc, *args)
    r = _run(nc, [arrays], core_ids=[0])
    return r.results[0]["out_0_dram"]
```
